# Optimizing a Trainium2 kernel written in Bass

```python
import numpy as np
import jax
import jax.numpy as jnp

def _softmax(x, axis=-1):
    return jax.nn.softmax(x, axis=axis)

def _gelu(x):
    return jax.nn.gelu(x, approximate=True)

def _silu(x):
    return jax.nn.silu(x)

def _sigmoid(x):
    return jax.nn.sigmoid(x)

def _layernorm(x, axis=-1, eps=1e-05):
    m = jnp.mean(x, axis=axis, keepdims=True)
    v = jnp.var(x, axis=axis, keepdims=True)
    return (x - m) / jnp.sqrt(v + eps)

def _scatter_add(tgt, idx, src, axis=0):
    return tgt.at[idx].add(src)

def _segment_sum(src, seg, n):
    return jax.ops.segment_sum(src, seg, n)
kernel_name = 'mk_prb_d1_jaxref_r4_26b9dd'

def setup_inputs(seed: int=0):
    np.random.seed(seed)
    _w = jnp.asarray

    def _L0_attn_setup():
        import jax, jax.numpy as jnp
        import numpy as np
        B, N, D, H = (2, 512, 256, 16)
        DH = D // H
        EPS = 1e-05

        def _lrpe(t, theta, n):
            idx = jnp.arange(n, dtype=t.dtype).reshape(1, n, 1)
            th = theta * idx
            return jnp.concatenate([t * jnp.cos(th), t * jnp.sin(th)], axis=-1)
        key = jax.random.key(seed)
        ks = jax.random.split(key, 8)
        x = jax.random.normal(ks[0], (B, N, D), dtype=jnp.float32)
        context = jax.random.normal(ks[1], (B, N, D), dtype=jnp.float32)
        Wqkvu = jax.random.normal(ks[2], (4 * D, D), dtype=jnp.float32) * 0.02
        bqkvu = jax.random.normal(ks[3], (4 * D,), dtype=jnp.float32) * 0.02
        Wout = jax.random.normal(ks[4], (D, D), dtype=jnp.float32) * 0.02
        bout = jax.random.normal(ks[5], (D,), dtype=jnp.float32) * 0.02
        theta = (10000.0 ** (-2.0 / D * jnp.arange(D, dtype=jnp.float32))).reshape(H, 1, DH)
        ln_w = jnp.ones((D,), dtype=jnp.float32)
        ln_b = jnp.zeros((D,), dtype=jnp.float32)
        return {'x': x, 'context': context, 'Wqkvu': Wqkvu, 'bqkvu': bqkvu, 'Wout': Wout, 'bout': bout, 'theta': theta, 'ln_w': ln_w, 'ln_b': ln_b}
    _L0_attn_in = _L0_attn_setup()

    def _L0_ffn_setup():
        import jax, jax.numpy as jnp
        import numpy as np
        DIM = 256

        def _reference_tuple_inner(x, W_r, W_k, W_v, mu_r, mu_k):
            B, T, C = x.shape
            x_prev = jnp.concatenate([jnp.zeros((B, 1, C), x.dtype), x[:, :-1, :]], axis=1)
            xr = mu_r * x + (1.0 - mu_r) * x_prev
            xk = mu_k * x + (1.0 - mu_k) * x_prev
            r = jax.nn.sigmoid(jnp.einsum('btc,dc->btd', xr, W_r))
            k = jnp.einsum('btc,dc->btd', xk, W_k)
            k_act = jnp.square(jax.nn.relu(k))
            out = r * jnp.einsum('btc,dc->btd', k_act, W_v)
            new_state = x[:, -1, :]
            return (out, new_state)
        key = jax.random.key(seed)
        ks = jax.random.split(key, 6)
        B, T, C = (8, 512, DIM)
        x = jax.random.normal(ks[0], (B, T, C), dtype=jnp.float32)
        s = 1.0 / np.sqrt(C)
        W_r = jax.random.uniform(ks[1], (C, C), jnp.float32, -s, s)
        W_k = jax.random.uniform(ks[2], (C, C), jnp.float32, -s, s)
        W_v = jax.random.uniform(ks[3], (C, C), jnp.float32, -s, s)
        mu_r = jax.random.uniform(ks[4], (C,), jnp.float32)
        mu_k = jax.random.uniform(ks[5], (C,), jnp.float32)
        return {'x': x, 'W_r': W_r, 'W_k': W_k, 'W_v': W_v, 'mu_r': mu_r, 'mu_k': mu_k}
    _L0_ffn_in = _L0_ffn_setup()
    _d = {'L0_attn_x': _L0_attn_in['x'], 'L0_attn_context': _L0_attn_in['context'], 'L0_attn_Wqkvu': _L0_attn_in['Wqkvu'], 'L0_attn_bqkvu': _L0_attn_in['bqkvu'], 'L0_attn_Wout': _L0_attn_in['Wout'], 'L0_attn_bout': _L0_attn_in['bout'], 'L0_attn_theta': _L0_attn_in['theta'], 'L0_attn_ln_w': _L0_attn_in['ln_w'], 'L0_attn_ln_b': _L0_attn_in['ln_b'], 'L0_ffn_W_r': _L0_ffn_in['W_r'], 'L0_ffn_W_k': _L0_ffn_in['W_k'], 'L0_ffn_W_v': _L0_ffn_in['W_v'], 'L0_ffn_mu_r': _L0_ffn_in['mu_r'], 'L0_ffn_mu_k': _L0_ffn_in['mu_k']}
    _x0 = _d['L0_attn_x']
    _d['L0_attn_x'] = jax.random.normal(jax.random.fold_in(jax.random.key(seed), 1), (2, 2048, 256), dtype=_x0.dtype)
    del _x0
    return _d

def reference(L0_attn_x, L0_attn_context, L0_attn_Wqkvu, L0_attn_bqkvu, L0_attn_Wout, L0_attn_bout, L0_attn_theta, L0_attn_ln_w, L0_attn_ln_b, L0_ffn_W_r, L0_ffn_W_k, L0_ffn_W_v, L0_ffn_mu_r, L0_ffn_mu_k):

    def _L0_attn_ref(x, context, Wqkvu, bqkvu, Wout, bout, theta, ln_w, ln_b):
        import jax, jax.numpy as jnp
        import numpy as np
        B, N, D, H = (2, 512, 256, 16)
        DH = D // H
        EPS = 1e-05

        def _lrpe(t, theta, n):
            idx = jnp.arange(n, dtype=t.dtype).reshape(1, n, 1)
            th = theta * idx
            return jnp.concatenate([t * jnp.cos(th), t * jnp.sin(th)], axis=-1)
        b, n, d = x.shape
        qkvu = x @ Wqkvu.T + bqkvu
        q, k, v, u = jnp.split(qkvu, 4, axis=-1)
        tohead = lambda t: t.reshape(b, n, H, DH).transpose(0, 2, 1, 3)
        q, k, v = (tohead(q), tohead(k), tohead(v))
        q = jax.nn.silu(q)
        k = jax.nn.silu(k)
        q = _lrpe(q, theta, n)
        k = _lrpe(k, theta, n)
        qk = jnp.einsum('bhmd,bhnd->bhmn', q, k)
        out = jnp.einsum('bhmn,bhne->bhme', qk, v)
        out = out.transpose(0, 2, 1, 3).reshape(b, n, d)
        mu = jnp.mean(out, axis=-1, keepdims=True)
        var = jnp.var(out, axis=-1, keepdims=True)
        out = (out - mu) * jax.lax.rsqrt(var + EPS) * ln_w + ln_b
        out = u * out
        return out @ Wout.T + bout

    def _L0_ffn_ref(x, W_r, W_k, W_v, mu_r, mu_k):
        import jax, jax.numpy as jnp
        import numpy as np
        DIM = 256

        def _reference_tuple_inner(x, W_r, W_k, W_v, mu_r, mu_k):
            B, T, C = x.shape
            x_prev = jnp.concatenate([jnp.zeros((B, 1, C), x.dtype), x[:, :-1, :]], axis=1)
            xr = mu_r * x + (1.0 - mu_r) * x_prev
            xk = mu_k * x + (1.0 - mu_k) * x_prev
            r = jax.nn.sigmoid(jnp.einsum('btc,dc->btd', xr, W_r))
            k = jnp.einsum('btc,dc->btd', xk, W_k)
            k_act = jnp.square(jax.nn.relu(k))
            out = r * jnp.einsum('btc,dc->btd', k_act, W_v)
            new_state = x[:, -1, :]
            return (out, new_state)
        return _reference_tuple_inner(x, W_r, W_k, W_v, mu_r, mu_k)[0]
    x = L0_attn_x
    xn = _layernorm(x, axis=-1)
    x = x + _L0_attn_ref(xn, L0_attn_context, L0_attn_Wqkvu, L0_attn_bqkvu, L0_attn_Wout, L0_attn_bout, L0_attn_theta, L0_attn_ln_w, L0_attn_ln_b) + _L0_ffn_ref(xn, L0_ffn_W_r, L0_ffn_W_k, L0_ffn_W_v, L0_ffn_mu_r, L0_ffn_mu_k)
    return x

_drawn_inputs = setup_inputs


def setup_inputs(seed=0):
    import zlib

    import numpy as np

    out = dict(_drawn_inputs(seed))
    spreads = {'L0_attn_ln_w': (1.0, 0.6), 'L0_attn_ln_b': (0.0, 0.754)}
    factors = {'L0_attn_bqkvu': 2.781, 'L0_attn_bout': 2.728, 'L0_ffn_W_r': 3.186, 'L0_ffn_mu_r': 6.408}
    for name, (base, spread) in spreads.items():
        noise = np.random.default_rng([zlib.crc32(name.encode()), seed]).standard_normal(out[name].shape)
        drawn = base * np.exp(spread * noise) if base else spread * noise
        out[name] = jnp.asarray(drawn.astype(out[name].dtype))
    for name, factor in factors.items():
        out[name] = (out[name] * factor).astype(out[name].dtype)
    return out
```

```python
from contextlib import ExitStack

import concourse.bass as bass
import numpy as np
from concourse import mybir

F32 = mybir.dt.float32
F32R = mybir.dt.float32r
U32 = mybir.dt.uint32
ALU = mybir.AluOpType
ACT = mybir.ActivationFunctionType

P = 128
EPS = 1e-5
TWO_PI_HI = 6.28125
TWO_PI_LO = float(np.float32(2 * np.pi - 6.28125))
INV_TWO_PI = float(np.float32(1 / (2 * np.pi)))
ROUND = float(1.5 * 2**23)
PI_BELOW = 3.1415925


def lrpe_block_kernel(nc, x, w_qkvu_t, b_qkvu, w_out_t, b_out, theta, ln_w, ln_b,
                      w_r_t, w_k_t, w_v_t, mu_r, mu_k, consts, out):
    B, N, D = x.shape
    C = D // P
    BLK = 512
    T = BLK // P
    NP = N // BLK
    NT = N // P
    G = 64
    SMALL_LOADS = 9
    assert B == 2 and D == 2 * P and T == 4

    x_v = x.rearrange("b (p t i) c -> b p i t c", t=T, i=P)
    out_v = out.rearrange("b (p t i) c -> b p i t c", t=T, i=P)

    with ExitStack() as ctx:
        def sb(name, shape, dt=F32, stack=None):
            return (stack or ctx).enter_context(nc.sbuf_tensor(name, shape, dt))

        def sem(name):
            return ctx.enter_context(nc.semaphore(name))

        xn_t = sb("xn_t", [P, C, B, 1 + N])
        q_t = sb("q_t", [P, C, B, N])
        u_t = sb("u_t", [P, C, B, N])
        rot_t = sb("rot_t", [P, 2, C, N])
        const = sb("const", [P, P + G + NT])
        cols = sb("cols", [P, 6 * C])
        neg_half = sb("neg_half", [P, T])
        neg_one = sb("neg_one", [P, T])
        eps = sb("eps", [P, T])
        half_pi = sb("half_pi", [P, 1])
        tick = sb("tick", [P, 1])
        stats = sb("stats", [P, T, 6])
        mv = sb("mv", [P, 2, T, 2])
        rstd = sb("rstd", [P, 2, T])
        nmr = sb("nmr", [P, 2, T])
        ident, mask, pos = const[:, 0:P], const[:, P:P + G], const[:, P + G:P + G + NT]
        bq, bu, lnw, lnb, mur, muk = (cols[:, C * i:C * i + C] for i in range(6))

        one = ExitStack()
        angle = sb("angle", [P, 2, T, D], stack=one)
        w_hi = sb("w_hi", [P, C, 4 * D], F32R, stack=one)
        w_lo = sb("w_lo", [P, C, 4 * D], F32R, stack=one)
        xn_hi = sb("xn_hi", [P, B, C, BLK], F32R, stack=one)
        xn_lo = sb("xn_lo", [P, B, C, BLK], F32R, stack=one)
        x_in = sb("x_in", [P, B, T, D], stack=one)
        rot = sb("rot", [P, 2, T, D], stack=one)
        k_silu = sb("k_silu", [P, T, D], stack=one)
        k_rot = sb("k_rot", [P, T, 2, D], stack=one)
        v_sb = sb("v_sb", [P, T, D], stack=one)
        theta_bc = sb("theta_bc", [P, D], stack=one)
        b_row = sb("b_row", [P, 2 * D], F32R, stack=one)
        ones_r = sb("ones_r", [P, P], F32R, stack=one)
        kv_acc = sb("kv_acc", [P, B, C, 2, G], stack=one)
        one.close()
        w_raw = u_t[:, 0, 0, 0:C * 4 * D].rearrange("p (c n) -> p c n", c=C)
        b_raw = q_t[0:1, 0, 0, 0:2 * D]

        two = ExitStack()
        w_mix = sb("w_mix", [P, 4, C, D], stack=two)
        kv_bd = sb("kv_bd", [P, B, 2, C, P], stack=two)
        q_rot = sb("q_rot", [P, 2, C, BLK], stack=two)
        x_r = sb("x_r", [P, C, BLK], stack=two)
        x_k = sb("x_k", [P, C, BLK], stack=two)
        diff = sb("diff", [P, C, BLK], stack=two)
        k_relu = sb("k_relu", [P, BLK], stack=two)
        k_act = sb("k_act", [P, C, BLK], stack=two)
        z = sb("z", [P, T, D], stack=two)
        z_aff = sb("z_aff", [P, C, BLK], stack=two)
        gated = sb("gated", [P, C, BLK], stack=two)
        r_tanh = sb("r_tanh", [P, 2, D], stack=two)
        y = sb("y", [P, B, T, D], stack=two)
        x_res = sb("x_res", [P, T, D], stack=two)
        b_out_bc = sb("b_out_bc", [P, D], stack=two)
        two.close()

        bank = [ctx.enter_context(nc.psum_tensor(f"bank{i}", [P, BLK], F32)) for i in range(4)]
        pair_a = ctx.enter_context(nc.psum_tensor("pair_a", [P, 2, BLK], F32))
        pair_b = ctx.enter_context(nc.psum_tensor("pair_b", [P, 2, BLK], F32))
        k_ps, v_ps, rot_ps, kv_ps = bank
        xn_ps, qu_ps = pair_a, pair_b
        r_ps, kf_ps, vf_ps, w_ps = bank
        o_ps, z_ps = pair_a, pair_b

        x_loaded = [sem(f"x_loaded{b}") for b in range(B)]
        w_loaded = sem("w_loaded")
        small_loaded = sem("small_loaded")
        mix_loaded = sem("mix_loaded")
        bout_loaded = sem("bout_loaded")
        zeroed = sem("zeroed")
        theta_ready = sem("theta_ready")
        w_hi_ready, w_lo_ready = sem("w_hi_ready"), sem("w_lo_ready")
        dve_step = sem("dve_step")
        pool_step = sem("pool_step")
        stats_ready = sem("stats_ready")
        angle_step = sem("angle_step")
        half_wv = sem("half_wv")
        mv_ready, rstd_ready = sem("mv_ready"), sem("rstd_ready")
        xn_ready = sem("xn_ready")
        xn_transposed = sem("xn_transposed")
        xn_t_ready = sem("xn_t_ready")
        split_ready = sem("split_ready")
        k_proj, v_proj = sem("k_proj"), sem("v_proj")
        k_silu_ready, v_ready = sem("k_silu_ready"), sem("v_ready")
        q_proj, u_proj = sem("q_proj"), sem("u_proj")
        q_ready, u_ready = sem("q_ready"), sem("u_ready")
        k_rot_ready = sem("k_rot_ready")
        kv_done, kv_added = sem("kv_done"), sem("kv_added")
        angle_ready = sem("angle_ready")
        rot_ready = sem("rot_ready")
        rot_transposed, rot_t_ready = sem("rot_transposed"), sem("rot_t_ready")
        kv_bd_zeroed = sem("kv_bd_zeroed")
        kv_turned, kv_bd_ready = sem("kv_turned"), sem("kv_bd_ready")
        diff_ready = sem("diff_ready")
        xk_ready, xr_ready = sem("xk_ready"), sem("xr_ready")
        q_rot_ready = sem("q_rot_ready")
        o_done = sem("o_done")
        mv2_ready, rstd2_ready = sem("mv2_ready"), sem("rstd2_ready")
        z_ready = sem("z_ready")
        z_transposed = sem("z_transposed")
        aff_ready, gated_ready = sem("aff_ready"), sem("gated_ready")
        kf_done, relu_done, k_act_ready = sem("kf_done"), sem("relu_done"), sem("k_act_ready")
        r_done, tanh_ready = sem("r_done"), sem("tanh_ready")
        vf_done, rv_ready = sem("vf_done"), sem("rv_ready")
        w_done, y_ready = sem("w_done"), sem("y_ready")
        res_loaded = sem("res_loaded")
        xb_ready, y_part = sem("xb_ready"), sem("y_part")
        stored = [sem(f"stored{b}") for b in range(B)]

        block = ctx.enter_context(nc.Block())

        def turns(eng, body):
            body(0, False)
            with eng.Fori(1, NP - 1) as p:
                body(p, False)
            body(NP - 1, True)

        def wait_for(eng, semaphore, count):
            if not (isinstance(count, int) and count <= 0):
                eng.wait_ge(semaphore, count)

        def unit(p, b):
            return 2 * p + b

        def next_unit(p, b):
            return (p, 1) if b == 0 else (p + 1, 0)

        def tokens(p, shift=0):
            return bass.ds(p * BLK + shift, BLK)

        @block.sync
        def _(sp):
            for b in range(B):
                sp.dma_start(x_in[:, b], x_v[b, 0]).then_inc(x_loaded[b], 16)
                if b == 0:
                    for c in range(C):
                        sp.dma_start(w_raw[:, c], w_qkvu_t[c * P:(c + 1) * P, :]).then_inc(w_loaded, 16)

            def load_x(p, last):
                for b in range(B):
                    sp.wait_ge(xn_transposed, unit(p, b) + 1)
                    sp.dma_start(x_in[:, b], x_v[b, bass.ds(p + 1, 1)].rearrange("o i t c -> i (o t) c")
                                 ).then_inc(x_loaded[b], 16)

            load_x(0, False)
            with sp.Fori(1, NP - 1) as p:
                load_x(p, False)
            sp.wait_ge(rot_ready, 2 * NP)
            for i, w in enumerate((w_r_t, w_k_t, w_v_t, w_out_t)):
                sp.dma_start(w_mix[:, i], w.rearrange("(c p) n -> p c n", p=P)).then_inc(mix_loaded, 16)

            sp.wait_ge(kv_added, B * NP)
            sp.dma_start(b_out_bc[:], b_out.to_broadcast([P, D])).then_inc(bout_loaded, 16)

            def store(p, last):
                for b in range(B):
                    u = unit(p, b)
                    wait_for(sp, y_part, 2 * u)
                    sp.dma_start(x_res[:], x_v[b, bass.ds(p, 1)].rearrange("o i t c -> i (o t) c")
                                 ).then_inc(res_loaded, 16)
                    sp.wait_ge(y_ready, 2 * u + 2)
                    sp.dma_start(out_v[b, bass.ds(p, 1)].rearrange("o i t c -> i (o t) c"), y[:, b]
                                 ).then_inc(stored[b], 16)

            turns(sp, store)
            for b in range(B):
                sp.wait_ge(stored[b], 16 * NP)

        @block.gpsimd
        def _(pool):
            nc.gpsimd.memset(neg_half[:], -0.5).then_inc(pool_step, 1)
            nc.gpsimd.memset(kv_acc[:], 0.0).then_inc(zeroed, 1)
            nc.gpsimd.memset(xn_t[:, :, :, 0:1], 0.0).then_inc(zeroed, 1)
            nc.gpsimd.memset(neg_one[:], -1.0).then_inc(pool_step, 1)
            nc.gpsimd.memset(eps[:], EPS).then_inc(pool_step, 1)
            pool.wait_ge(pool_step, 3)

            def rstd_of(b, ready, base):
                nc.gpsimd.tensor_tensor(rstd[:, b], mv[:, b, :, 1], eps[:], ALU.add).then_inc(pool_step, 1)
                nc.gpsimd.tensor_tensor(nmr[:, b], mv[:, b, :, 0], neg_one[:], ALU.mult).then_inc(pool_step, 1)
                pool.wait_ge(pool_step, base + 2)
                nc.gpsimd.tensor_tensor(rstd[:, b], rstd[:, b], neg_half[:], ALU.pow).then_inc(pool_step, 1)
                pool.wait_ge(pool_step, base + 3)
                nc.gpsimd.tensor_tensor(nmr[:, b], nmr[:, b], rstd[:, b], ALU.mult).then_inc(ready, 1)

            def one_unit(p, b):
                u = unit(p, b)
                pool.wait_ge(mv_ready, u + 1)
                rstd_of(b, rstd_ready, 3 + 3 * u)

            def phase1(p, last):
                for b in range(B):
                    one_unit(p, b)

            turns(pool, phase1)
            pool.wait_ge(u_proj, 2 * B * NP)
            nc.gpsimd.memset(kv_bd[:], 0.0).then_inc(kv_bd_zeroed, 1)
            pool.wait_ge(kv_added, B * NP)
            pool.wait_ge(xn_t_ready, B * NP)

            def make_diff(p, b, u):
                wait_for(pool, xr_ready, C * u)
                nc.gpsimd.tensor_tensor(diff[:], xn_t[:, :, b, tokens(p, 1)], xn_t[:, :, b, tokens(p)],
                                        ALU.subtract).then_inc(diff_ready, 1)

            make_diff(0, 0, 0)
            pool.wait_ge(bout_loaded, 16)

            def phase2(p, last):
                for b in range(B):
                    u = unit(p, b)
                    pool.wait_ge(res_loaded, 16 * (u + 1))
                    nc.gpsimd.tensor_tensor(x_res[:], x_res[:], b_out_bc[:].unsqueeze(1).to_broadcast([P, T, D]),
                                            ALU.add).then_inc(xb_ready, 1)
                    pool.wait_ge(mv2_ready, u + 1)
                    rstd_of(b, rstd2_ready, 3 + 3 * B * NP + 3 * u)
                    pool.wait_ge(xb_ready, u + 1)
                    for j in range(2):
                        pool.wait_ge(rv_ready, 2 * u + j + 1)
                        nc.gpsimd.tensor_tensor(y[:, b, 2 * j:2 * j + 2], y[:, b, 2 * j:2 * j + 2],
                                                x_res[:, 2 * j:2 * j + 2], ALU.add).then_inc(y_part, 1)
                        if j == 0 and not (last and b == 1):
                            make_diff(*next_unit(p, b), u + 1)

            turns(pool, phase2)

        @block.scalar
        def _(act):
            act.dma_start(const[:], consts).then_inc(small_loaded, 16)
            act.dma_start(theta_bc[:], theta.to_broadcast([P, D])).then_inc(small_loaded, 16)
            act.dma_start(b_raw, b_qkvu[:, 0:2 * D]).then_inc(small_loaded, 16)
            bq_v = b_qkvu[:, 2 * D:3 * D].rearrange("o (c p) -> p (o c)", p=P)
            bu_v = b_qkvu[:, 3 * D:4 * D].rearrange("o (c p) -> p (o c)", p=P)
            col = lambda a: a.rearrange("o (c p) -> p (o c)", p=P)
            with nc.allow_non_contiguous_dma(reason="six columns of a few hundred bytes"):
                for dst, src in ((bq, bq_v), (bu, bu_v), (lnw, col(ln_w)), (lnb, col(ln_b)),
                                 (mur, col(mu_r)), (muk, col(mu_k))):
                    act.dma_start(dst, src).then_inc(small_loaded, 16)
            act.wait_ge(w_loaded, 16 * C)
            nc.scalar.activation(w_hi[:, :, 0:2 * D], w_raw[:, :, 0:2 * D], ACT.Copy).then_inc(w_hi_ready, 1)
            nc.scalar.activation(w_hi[:, :, 2 * D:], w_raw[:, :, 2 * D:], ACT.Copy).then_inc(w_hi_ready, 1)

            def keep_xn_t(p, b, u):
                act.wait_ge(xn_transposed, u + 1)
                nc.scalar.activation(xn_t[:, :, b, tokens(p, 1)], xn_ps[:], ACT.Copy).then_inc(xn_t_ready, 1)

            def sin_cos(n):
                act.wait_ge(angle_ready, n + 1)
                nc.scalar.activation(rot[:, 1], angle[:, 0], ACT.Sin).then_inc(rot_ready, 1)
                nc.scalar.activation(rot[:, 0], angle[:, 1], ACT.Sin, bias=half_pi[:], scale=-1.0).then_inc(rot_ready, 1)

            def keep_rot_t(p, j, count):
                act.wait_ge(rot_transposed, count + 1)
                nc.scalar.activation(rot_t[:, j // C, j % C, tokens(p)], rot_ps[:], ACT.Copy).then_inc(rot_t_ready, 1)

            act.wait_ge(zeroed, 4)
            keep_xn_t(0, 0, 0)
            sin_cos(0)
            act.wait_ge(small_loaded, 16 * SMALL_LOADS)
            act.wait_ge(w_hi_ready, 2)
            act.wait_ge(w_lo_ready, 3)

            def phase1(p, last):
                for b in range(B):
                    u = unit(p, b)
                    for j in range(2):
                        act.wait_ge(k_proj, 2 * u + j + 1)
                        if j == 0:
                            wait_for(act, k_rot_ready, 2 * u)
                        nc.scalar.activation(k_silu[:, 2 * j:2 * j + 2], k_ps[:].rearrange("p (t n) -> p t n", t=2),
                                             ACT.Silu).then_inc(k_silu_ready, 1)
                        act.wait_ge(v_proj, 2 * u + j + 1)
                        if j == 0:
                            wait_for(act, kv_done, u)
                        nc.scalar.activation(v_sb[:, 2 * j:2 * j + 2], v_ps[:].rearrange("p (t n) -> p t n", t=2),
                                             ACT.Copy).then_inc(v_ready, 1)
                    keep_rot_t(p, 2 * b, 4 * p + 2 * b)
                    if not (last and b == 1):
                        keep_xn_t(*next_unit(p, b), u + 1)
                    for c in range(C):
                        act.wait_ge(q_proj, 2 * u + c + 1)
                        nc.scalar.activation(q_t[:, c, b, tokens(p)], qu_ps[:, c], ACT.Silu, bias=bq[:, c:c + 1]
                                             ).then_inc(q_ready, 1)
                    for c in range(C):
                        act.wait_ge(u_proj, 2 * u + c + 1)
                        nc.scalar.activation(u_t[:, c, b, tokens(p)], qu_ps[:, c], ACT.Identity, bias=bu[:, c:c + 1]
                                             ).then_inc(u_ready, 1)
                    keep_rot_t(p, 2 * b + 1, 4 * p + 2 * b + 1)
                if not last:
                    act.wait_ge(k_rot_ready, 2 * unit(p, 1) + 2)
                    sin_cos(p + 1)

            turns(act, phase1)

            def phase2(p, last):
                for b in range(B):
                    u = unit(p, b)
                    for c in range(C):
                        act.wait_ge(kf_done, 2 * u + c + 1)
                        wait_for(act, k_act_ready, 2 * u + c)
                        nc.scalar.activation(k_relu[:], kf_ps[:], ACT.Relu).then_inc(relu_done, 1)
                        act.wait_ge(relu_done, 2 * u + c + 1)
                        if c == 0:
                            wait_for(act, vf_done, 2 * u)
                        nc.scalar.activation(k_act[:, c], k_relu[:], ACT.Square).then_inc(k_act_ready, 1)
                    act.wait_ge(r_done, 2 * u + 1)
                    wait_for(act, rv_ready, 2 * u)
                    nc.scalar.activation(r_tanh[:], r_ps[:].rearrange("p (t n) -> p t n", t=2), ACT.Tanh, scale=0.5
                                         ).then_inc(tanh_ready, 1)
                    act.wait_ge(rstd2_ready, u + 1)
                    wait_for(act, z_transposed, u)
                    for t in range(T):
                        ins = nc.scalar.activation(z[:, t], o_ps[:, t // 2, (t % 2) * D:(t % 2 + 1) * D], ACT.Identity,
                                                   bias=nmr[:, b, t:t + 1], scale=rstd[:, b, t:t + 1])
                    ins.then_inc(z_ready, 1)
                    for c in range(C):
                        if c == 0:
                            act.wait_ge(z_transposed, u + 1)
                            wait_for(act, gated_ready, 2 * u)
                        nc.scalar.activation(z_aff[:, c], z_ps[:, c], ACT.Identity, bias=lnb[:, c:c + 1],
                                             scale=lnw[:, c:c + 1]).then_inc(aff_ready, 1)
                    act.wait_ge(r_done, 2 * u + 2)
                    act.wait_ge(rv_ready, 2 * u + 1)
                    nc.scalar.activation(r_tanh[:], r_ps[:].rearrange("p (t n) -> p t n", t=2), ACT.Tanh, scale=0.5
                                         ).then_inc(tanh_ready, 1)

            act.wait_ge(kv_added, B * NP)
            turns(act, phase2)

        @block.vector
        def _(dve):
            count = [0]

            def then(ins):
                count[0] += 1
                ins.then_inc(dve_step, 1)
                dve.wait_ge(dve_step, count[0])

            nc.vector.memset(half_pi[:], float(np.float32(np.pi / 2))).then_inc(zeroed, 1)
            nc.vector.memset(ones_r[:].bitcast(F32), 1.0).then_inc(zeroed, 1)
            then(nc.vector.memset(b_row[:].bitcast(F32), 0.0))

            def statistics(p, b, u, ready, src):
                for t in range(T):
                    ins = nc.vector.bn_stats(stats[:, t], src(t))
                return ins

            def stats1(p, b, u):
                dve.wait_ge(x_loaded[b], 16 * (p + 1))
                for t in range(T):
                    nc.vector.bn_stats(stats[:, t], x_in[:, b, t]).then_inc(stats_ready, 1)
                dve.wait_ge(stats_ready, T * (u + 1))
                nc.vector.memset(tick[:], 0.0)
                for t in range(T):
                    ins = nc.vector.bn_aggr(mv[:, b, t], stats[:, t])
                ins.then_inc(mv_ready, 1)

            def norm1(b, u):
                dve.wait_ge(rstd_ready, u + 1)
                for t in range(T):
                    ins = nc.vector.tensor_scalar(x_in[:, b, t], x_in[:, b, t], mv[:, b, t, 0:1], rstd[:, b, t:t + 1],
                                                  ALU.subtract, ALU.mult)
                ins.then_inc(xn_ready, 1)

            def split(p, b, u):
                dve.wait_ge(xn_t_ready, u + 1)
                wait_for(dve, u_proj, 2 * (u - 1))
                nc.vector.tensor_copy(xn_hi[:, b], xn_t[:, :, b, tokens(p, 1)]).then_inc(split_ready, 1)
                dve.wait_ge(split_ready, 2 * u + 1)
                nc.vector.tensor_tensor(xn_lo[:, b], xn_t[:, :, b, tokens(p, 1)], xn_hi[:, b].bitcast(F32),
                                        ALU.subtract).then_inc(split_ready, 1)

            ANGLE_STEPS = 7

            def angles_a(n):
                wait_for(dve, rot_ready, 2 * n)
                a, k = angle[:, 0], angle[:, 1]
                nc.vector.tensor_tensor(a, theta_bc[:].unsqueeze(1).to_broadcast([P, T, D]),
                                        pos[:, bass.ds(n * T, T)].unsqueeze(2).to_broadcast([P, T, D]),
                                        ALU.mult).then_inc(angle_step, 1)
                dve.wait_ge(angle_step, ANGLE_STEPS * n + 1)
                nc.vector.tensor_scalar(k, a, INV_TWO_PI, ROUND, ALU.mult, ALU.add).then_inc(angle_step, 1)
                dve.wait_ge(angle_step, ANGLE_STEPS * n + 2)
                nc.vector.tensor_scalar(k, k, -ROUND, None, ALU.add).then_inc(angle_step, 1)
                dve.wait_ge(angle_step, ANGLE_STEPS * n + 3)
                nc.vector.scalar_tensor_tensor(a, k, -TWO_PI_HI, a, ALU.mult, ALU.add).then_inc(angle_step, 1)

            def angles_b(n):
                a, k = angle[:, 0], angle[:, 1]
                dve.wait_ge(angle_step, ANGLE_STEPS * n + 4)
                nc.vector.scalar_tensor_tensor(a, k, -TWO_PI_LO, a, ALU.mult, ALU.add).then_inc(angle_step, 1)
                dve.wait_ge(angle_step, ANGLE_STEPS * n + 5)
                nc.vector.tensor_scalar(a, a, PI_BELOW, -PI_BELOW, ALU.min, ALU.max).then_inc(angle_step, 1)
                dve.wait_ge(angle_step, ANGLE_STEPS * n + 6)
                nc.vector.tensor_scalar(k.bitcast(U32), a.bitcast(U32), 0x7FFFFFFF, None, ALU.bitwise_and).then_inc(angle_step, 1)
                dve.wait_ge(angle_step, ANGLE_STEPS * n + 7)
                nc.vector.memset(tick[:], 0.0).then_inc(angle_ready, 1)

            def rotate_k(u, j, b):
                dve.wait_ge(k_silu_ready, 2 * u + j + 1)
                if j == 0:
                    wait_for(dve, kv_done, u)
                for cs in range(2):
                    ins = nc.vector.tensor_tensor(k_rot[:, 2 * j:2 * j + 2, cs], k_silu[:, 2 * j:2 * j + 2],
                                                  rot[:, cs, 2 * j:2 * j + 2], ALU.mult)
                ins.then_inc(k_rot_ready, 1)

            def add_kv(b, u):
                dve.wait_ge(kv_done, u + 1)
                nc.vector.tensor_tensor(kv_acc[:, b], kv_acc[:, b],
                                        kv_ps[:, 0:C * 2 * G].rearrange("p (c s g) -> p c s g", c=C, s=2),
                                        ALU.add).then_inc(kv_added, 1)

            stats1(0, 0, 0)
            dve.wait_ge(w_hi_ready, 1)
            nc.vector.tensor_tensor(w_lo[:, :, 0:2 * D], w_raw[:, :, 0:2 * D], w_hi[:, :, 0:2 * D].bitcast(F32),
                                    ALU.subtract).then_inc(w_lo_ready, 1)
            norm1(0, 0)
            dve.wait_ge(small_loaded, 16 * SMALL_LOADS)
            then(nc.vector.tensor_copy(b_row[0:1], b_raw))
            nc.vector.tensor_tensor(b_row[32:33], b_raw, b_row[0:1].bitcast(F32), ALU.subtract).then_inc(w_lo_ready, 1)
            stats1(0, 1, 1)
            split(0, 0, 0)
            dve.wait_ge(w_hi_ready, 2)
            nc.vector.tensor_tensor(w_lo[:, :, 2 * D:], w_raw[:, :, 2 * D:], w_hi[:, :, 2 * D:].bitcast(F32),
                                    ALU.subtract).then_inc(w_lo_ready, 1)
            angles_a(0)
            angles_b(0)
            dve.wait_ge(zeroed, 4)

            def phase1(p, last):
                for b in range(B):
                    u = unit(p, b)
                    end = last and b == 1
                    if not end:
                        norm1(next_unit(p, b)[1], u + 1)
                    if b == 0:
                        dve.wait_ge(rot_ready, 2 * p + 2)
                    rotate_k(u, 0, b)
                    rotate_k(u, 1, b)
                    if not end:
                        split(*next_unit(p, b), u + 1)
                    if not last:
                        stats1(p + 1, b, u + 2)
                        if b == 0:
                            angles_a(p + 1)
                        else:
                            angles_b(p + 1)
                    add_kv(b, u)

            turns(dve, phase1)

            dve.wait_ge(kv_bd_zeroed, 1)
            for b in range(B):
                dve.wait_ge(kv_turned, b + 1)
                turned = bank[b][:, 0:C * P].rearrange("p (c e) -> p c e", c=C)
                for cs in range(2):
                    for h in range(2):
                        rows, src, e = slice(G * h, G * h + G), slice(G * cs, G * cs + G), slice(G * h, G * h + G)
                        ins = nc.vector.tensor_tensor(kv_bd[rows, b, cs, :, e], turned[src, :, e],
                                                      mask[src].unsqueeze(1).to_broadcast([G, C, G]), ALU.mult)
                ins.then_inc(kv_bd_ready, 1)
            dve.wait_ge(mix_loaded, 16 * 4)
            nc.vector.tensor_scalar(w_mix[:, 2], w_mix[:, 2], 0.5, None, ALU.mult).then_inc(half_wv, 1)

            def rotate_q(p, b, u):
                wait_for(dve, o_done, 2 * u)
                for cs in range(2):
                    nc.vector.tensor_tensor(q_rot[:, cs], q_t[:, :, b, tokens(p)], rot_t[:, cs, :, tokens(p)],
                                            ALU.mult).then_inc(q_rot_ready, 1)

            def mixed(dst, mu, p, b, u, used, ready):
                dve.wait_ge(diff_ready, u + 1)
                wait_for(dve, used, 2 * u)
                for c in range(C):
                    nc.vector.scalar_tensor_tensor(dst[:, c], diff[:, c], mu[:, c:c + 1], xn_t[:, c, b, tokens(p)],
                                                   ALU.mult, ALU.add).then_inc(ready, 1)

            dve.wait_ge(q_ready, 2 * B * NP)
            dve.wait_ge(u_ready, 2 * B * NP)
            dve.wait_ge(rot_t_ready, 4 * NP)
            rotate_q(0, 0, 0)
            mixed(x_k, muk, 0, 0, 0, kf_done, xk_ready)
            mixed(x_r, mur, 0, 0, 0, r_done, xr_ready)

            def phase2(p, last):
                for b in range(B):
                    u = unit(p, b)
                    end = last and b == 1
                    for j in range(2):
                        dve.wait_ge(o_done, 2 * u + j + 1)
                        for i in range(2):
                            nc.vector.bn_stats(stats[:, 2 * j + i], o_ps[:, j, i * D:(i + 1) * D]).then_inc(stats_ready, 1)
                    dve.wait_ge(stats_ready, T * (B * NP + u + 1))
                    nc.vector.memset(tick[:], 0.0)
                    for t in range(T):
                        ins = nc.vector.bn_aggr(mv[:, b, t], stats[:, t])
                    ins.then_inc(mv2_ready, 1)
                    if not end:
                        rotate_q(*next_unit(p, b), u + 1)
                    def gate_v(j):
                        dve.wait_ge(vf_done, 2 * u + j + 1)
                        dve.wait_ge(tanh_ready, 2 * u + j + 1)
                        if j == 0:
                            wait_for(dve, stored[b], 16 * p)
                        nc.vector.scalar_tensor_tensor(y[:, b, 2 * j:2 * j + 2], r_tanh[:], 1.0,
                                                       vf_ps[:].rearrange("p (t n) -> p t n", t=2),
                                                       ALU.add, ALU.mult).then_inc(rv_ready, 1)

                    gate_v(0)
                    for c in range(C):
                        dve.wait_ge(aff_ready, 2 * u + c + 1)
                        if c == 0:
                            wait_for(dve, w_done, 2 * u)
                        nc.vector.tensor_tensor(gated[:, c], z_aff[:, c], u_t[:, c, b, tokens(p)],
                                                ALU.mult).then_inc(gated_ready, 1)
                    if not end:
                        mixed(x_k, muk, *next_unit(p, b), u + 1, kf_done, xk_ready)
                    gate_v(1)
                    for j in range(2):
                        dve.wait_ge(w_done, 2 * u + j + 1)
                        dve.wait_ge(y_part, 2 * u + j + 1)
                        nc.vector.tensor_tensor(y[:, b, 2 * j:2 * j + 2], w_ps[:].rearrange("p (t n) -> p t n", t=2),
                                                y[:, b, 2 * j:2 * j + 2], ALU.add).then_inc(y_ready, 1)
                    if not end:
                        mixed(x_r, mur, *next_unit(p, b), u + 1, r_done, xr_ready)

            turns(dve, phase2)

        @block.tensor
        def _(pe):
            K0, V0, Q0, U0 = 0, D, 2 * D, 3 * D

            def turn_xn(b, u):
                pe.wait_ge(xn_ready, u + 1)
                wait_for(pe, xn_t_ready, u)
                for c in range(C):
                    for t in range(T):
                        ins = nc.tensor.transpose(xn_ps[:, c, t * P:(t + 1) * P], x_in[:, b, t, c * P:(c + 1) * P], ident)
                ins.then_inc(xn_transposed, 1)

            def tile_pair(ps, b, j, w0):
                nc.tensor.matmul(ps[:], ones_r[:], b_row[:, w0:w0 + D].unsqueeze(1).to_broadcast([P, 2, D]),
                                 start=True, stop=False)
                for i in range(2):
                    t = 2 * j + i
                    for c in range(C):
                        for x_part, w_part in ((xn_hi, w_hi), (xn_hi, w_lo), (xn_lo, w_hi)):
                            ins = nc.tensor.matmul(ps[:, i * D:(i + 1) * D], x_part[:, b, c, t * P:(t + 1) * P],
                                                   w_part[:, c, w0:w0 + D], start=False,
                                                   stop=i == 1 and c == C - 1 and x_part is xn_lo)
                return ins

            def channels(ps, b, w0):
                for c in range(C):
                    for w_part, x_part in ((w_hi, xn_hi), (w_lo, xn_hi), (w_hi, xn_lo)):
                        ins = nc.tensor.matmul(ps, w_part[:, c, w0:w0 + P], x_part[:, b, c],
                                               start=c == 0 and w_part is w_hi and x_part is xn_hi,
                                               stop=c == C - 1 and x_part is xn_lo)
                return ins

            def turn_rot(j, count):
                wait_for(pe, rot_t_ready, count)
                for t in range(T):
                    ins = nc.tensor.transpose(rot_ps[:, t * P:(t + 1) * P],
                                              rot[:, j // C, t, (j % C) * P:(j % C + 1) * P], ident)
                ins.then_inc(rot_transposed, 1)

            pe.wait_ge(small_loaded, 16 * SMALL_LOADS)
            turn_xn(0, 0)
            pe.wait_ge(zeroed, 4)
            pe.wait_ge(w_hi_ready, 1)
            pe.wait_ge(w_lo_ready, 2)

            def phase1(p, last):
                for b in range(B):
                    u = unit(p, b)
                    pe.wait_ge(split_ready, 2 * u + 2)
                    for j in range(2):
                        wait_for(pe, k_silu_ready, 2 * u + j)
                        tile_pair(k_ps, b, j, K0).then_inc(k_proj, 1)
                        wait_for(pe, v_ready, 2 * u + j)
                        tile_pair(v_ps, b, j, V0).then_inc(v_proj, 1)
                    if b == 0:
                        pe.wait_ge(rot_ready, 2 * p + 2)
                    turn_rot(2 * b, 4 * p + 2 * b)
                    if not (last and b == 1):
                        turn_xn(next_unit(p, b)[1], u + 1)
                    pe.wait_ge(w_hi_ready, 2)
                    pe.wait_ge(w_lo_ready, 3)
                    for c in range(C):
                        wait_for(pe, u_ready, 2 * u)
                        channels(qu_ps[:, c], b, Q0 + c * P).then_inc(q_proj, 1)
                    for c in range(C):
                        pe.wait_ge(q_ready, 2 * u + c + 1)
                        channels(qu_ps[:, c], b, U0 + c * P).then_inc(u_proj, 1)
                    turn_rot(2 * b + 1, 4 * p + 2 * b + 1)
                    pe.wait_ge(v_ready, 2 * u + 2)
                    pe.wait_ge(k_rot_ready, 2 * u + 2)
                    wait_for(pe, kv_added, u)
                    for t in range(T):
                        for c in range(C):
                            for h in range(2):
                                d0 = c * P + h * G
                                ins = nc.tensor.matmul(
                                    kv_ps[h * G:(h + 1) * G, c * 2 * G:(c + 1) * 2 * G],
                                    v_sb[:, t, d0:d0 + G], k_rot[:, t, :, d0:d0 + G],
                                    start=t == 0 and c == 0, stop=t == T - 1, skip_group_check=True)
                    ins.then_inc(kv_done, 1)

            turns(pe, phase1)

            for b in range(B):
                pe.wait_ge(kv_added, B * NP)
                for c in range(C):
                    ins = nc.tensor.transpose(bank[b][:, c * P:(c + 1) * P],
                                              kv_acc[:, b, c].rearrange("p s g -> p (s g)"), ident)
                ins.then_inc(kv_turned, 1)

            W_R, W_K, W_V, W_O = range(4)

            def rows(ps, x_t, w, j):
                for i in range(2):
                    t = 2 * j + i
                    for c in range(C):
                        ins = nc.tensor.matmul(ps[:, i * D:(i + 1) * D], x_t[:, c, t * P:(t + 1) * P],
                                               w_mix[:, w, c], start=c == 0, stop=c == C - 1)
                return ins

            pe.wait_ge(mix_loaded, 16 * 4)
            pe.wait_ge(half_wv, 1)
            pe.wait_ge(kv_bd_ready, B)

            def phase2(p, last):
                for b in range(B):
                    u = unit(p, b)

                    def attend(j):
                        for i in range(2):
                            t = 2 * j + i
                            for c in range(C):
                                for cs in range(2):
                                    ins = nc.tensor.matmul(o_ps[:, j, i * D + c * P:i * D + (c + 1) * P],
                                                           q_rot[:, cs, c, t * P:(t + 1) * P], kv_bd[:, b, cs, c],
                                                           start=cs == 0, stop=cs == 1)
                        ins.then_inc(o_done, 1)

                    def mix_k(o):
                        wait_for(pe, relu_done, 2 * u + o)
                        for c in range(C):
                            ins = nc.tensor.matmul(kf_ps[:], w_mix[:, W_K, c, o * P:(o + 1) * P], x_k[:, c],
                                                   start=c == 0, stop=c == C - 1)
                        ins.then_inc(kf_done, 1)

                    pe.wait_ge(q_rot_ready, 2 * u + 2)
                    wait_for(pe, z_ready, u)
                    attend(0)
                    pe.wait_ge(xk_ready, 2 * u + 2)
                    mix_k(0)
                    attend(1)
                    mix_k(1)
                    pe.wait_ge(xr_ready, 2 * u + 2)
                    wait_for(pe, tanh_ready, 2 * u)
                    rows(r_ps, x_r, W_R, 0).then_inc(r_done, 1)
                    pe.wait_ge(k_act_ready, 2 * u + 2)
                    wait_for(pe, rv_ready, 2 * u)
                    rows(vf_ps, k_act, W_V, 0).then_inc(vf_done, 1)
                    pe.wait_ge(z_ready, u + 1)
                    wait_for(pe, aff_ready, 2 * u)
                    for c in range(C):
                        for t in range(T):
                            ins = nc.tensor.transpose(z_ps[:, c, t * P:(t + 1) * P], z[:, t, c * P:(c + 1) * P], ident)
                    ins.then_inc(z_transposed, 1)
                    pe.wait_ge(tanh_ready, 2 * u + 1)
                    rows(r_ps, x_r, W_R, 1).then_inc(r_done, 1)
                    pe.wait_ge(rv_ready, 2 * u + 1)
                    rows(vf_ps, k_act, W_V, 1).then_inc(vf_done, 1)
                    pe.wait_ge(gated_ready, 2 * u + 2)
                    wait_for(pe, y_ready, 2 * u)
                    rows(w_ps, gated, W_O, 0).then_inc(w_done, 1)
                    pe.wait_ge(y_ready, 2 * u + 1)
                    rows(w_ps, gated, W_O, 1).then_inc(w_done, 1)

            turns(pe, phase2)


def kernel(L0_attn_x, L0_attn_context, L0_attn_Wqkvu, L0_attn_bqkvu, L0_attn_Wout, L0_attn_bout, L0_attn_theta,
           L0_attn_ln_w, L0_attn_ln_b, L0_ffn_W_r, L0_ffn_W_k, L0_ffn_W_v, L0_ffn_mu_r, L0_ffn_mu_k):
    import concourse.bacc as bacc
    from concourse.bass_utils import run_bass_kernel_spmd

    x = np.ascontiguousarray(L0_attn_x)
    d = x.shape[2]
    order = [1, 2, 0, 3]
    w = np.asarray(L0_attn_Wqkvu).reshape(4, d, d)
    bias = np.asarray(L0_attn_bqkvu).reshape(4, d)
    n_tiles = x.shape[1] // P
    p_i = np.arange(P)[:, None]
    identity = (p_i == np.arange(P)[None, :]).astype(np.float32)
    mask = (p_i % 64 // 16 == np.arange(64)[None, :] // 16).astype(np.float32)
    positions = (p_i + P * np.arange(n_tiles)[None, :]).astype(np.float32)
    row = lambda a: np.ascontiguousarray(np.asarray(a).reshape(1, -1))
    arrays = {
        "x": x,
        "w_qkvu_t": np.ascontiguousarray(np.stack([w[i] for i in order]).reshape(4 * d, d).T),
        "b_qkvu": row(np.stack([bias[i] for i in order])),
        "w_out_t": np.ascontiguousarray(np.asarray(L0_attn_Wout).T),
        "b_out": row(L0_attn_bout),
        "theta": row(L0_attn_theta),
        "ln_w": row(L0_attn_ln_w),
        "ln_b": row(L0_attn_ln_b),
        "w_r_t": np.ascontiguousarray(np.asarray(L0_ffn_W_r).T),
        "w_k_t": np.ascontiguousarray(np.asarray(L0_ffn_W_k).T),
        "w_v_t": np.ascontiguousarray(np.asarray(L0_ffn_W_v).T),
        "mu_r": row(L0_ffn_mu_r),
        "mu_k": row(L0_ffn_mu_k),
        "consts": np.concatenate([identity, mask, positions], axis=1),
    }
    nc = bacc.Bacc("TRN2", target_bir_lowering=False, num_devices=1)
    args = [nc.dram_tensor(n, a.shape, mybir.dt.from_np(a.dtype), kind="ExternalInput").ap() for n, a in arrays.items()]
    out = nc.dram_tensor("out", x.shape, mybir.dt.from_np(x.dtype), kind="ExternalOutput").ap()
    lrpe_block_kernel(nc, *args, out)
    result = run_bass_kernel_spmd(nc, [arrays], core_ids=[0])
    return result.results[0]["out"]
```

```python
from contextlib import ExitStack

import concourse.bass as bass
import numpy as np
from concourse import mybir

F32 = mybir.dt.float32
F32R = mybir.dt.float32r
U32 = mybir.dt.uint32
ALU = mybir.AluOpType
ACT = mybir.ActivationFunctionType

P = 128
EPS = 1e-5
TWO_PI_HI = 6.28125
TWO_PI_LO = float(np.float32(2 * np.pi - 6.28125))
INV_TWO_PI = float(np.float32(1 / (2 * np.pi)))
ROUND = float(1.5 * 2**23)
PI_BELOW = 3.1415925


def lrpe_block_kernel(nc, x, w_qkvu_t, b_qkvu, w_out_t, b_out, theta, ln_w, ln_b,
                      w_r_t, w_k_t, w_v_t, mu_r, mu_k, consts, out):
    B, N, D = x.shape
    C = D // P
    BLK = 512
    T = BLK // P
    NP = N // BLK
    NT = N // P
    G = 64
    SMALL_LOADS = 8
    assert B == 2 and D == 2 * P and T == 4

    x_v = x.rearrange("b (p t i) c -> b p i t c", t=T, i=P)
    out_v = out.rearrange("b (p t i) c -> b p i t c", t=T, i=P)

    with ExitStack() as ctx:
        def sb(name, shape, dt=F32, stack=None):
            return (stack or ctx).enter_context(nc.sbuf_tensor(name, shape, dt))

        def sem(name):
            return ctx.enter_context(nc.semaphore(name))

        xn_t = sb("xn_t", [P, C, B, 1 + N])
        q_t = sb("q_t", [P, C, B, N])
        rot_t = sb("rot_t", [P, 2, C, N])
        mix_hi = sb("mix_hi", [P, 4, C, D], F32R)
        mix_lo = sb("mix_lo", [P, 4, C, D], F32R)
        const = sb("const", [P, P + G + NT])
        cols = sb("cols", [P, 6 * C])
        b_out_bc = sb("b_out_bc", [P, D])
        neg_half = sb("neg_half", [P, T])
        neg_one = sb("neg_one", [P, T])
        eps = sb("eps", [P, T])
        half_pi = sb("half_pi", [P, 1])
        tick = sb("tick", [P, 1])
        stats = sb("stats", [P, T, 6])
        mv = sb("mv", [P, 2, T, 2])
        rstd = sb("rstd", [P, 2, T])
        nmr = sb("nmr", [P, 2, T])
        ident, mask, pos = const[:, 0:P], const[:, P:P + G], const[:, P + G:P + G + NT]
        bq, bu, lnw, lnb, mur, muk = (cols[:, C * i:C * i + C] for i in range(6))

        one = ExitStack()
        angle = sb("angle", [P, 2, T, D], stack=one)
        w_stage = sb("w_stage", [P, C * 4 * D], stack=one)
        w_hi = sb("w_hi", [P, C, 4 * D], F32R, stack=one)
        w_lo = sb("w_lo", [P, C, 4 * D], F32R, stack=one)
        xn_hi = sb("xn_hi", [P, B, C, BLK], F32R, stack=one)
        xn_lo = sb("xn_lo", [P, B, C, BLK], F32R, stack=one)
        x_in = sb("x_in", [P, B, T, D], stack=one)
        rot = sb("rot", [P, 2, T, D], stack=one)
        k_silu = sb("k_silu", [P, T, D], stack=one)
        k_rot = sb("k_rot", [P, T, 2, D], stack=one)
        v_sb = sb("v_sb", [P, T, D], stack=one)
        u_out = sb("u_out", [P, B, C, BLK], stack=one)
        theta_bc = sb("theta_bc", [P, D], stack=one)
        b_v_bc = sb("b_v_bc", [P, D], stack=one)
        b_row = sb("b_row", [P, D], F32R, stack=one)
        ones_r = sb("ones_r", [P, P], F32R, stack=one)
        kv_acc = sb("kv_acc", [P, B, C, 2, G], stack=one)
        one.close()
        w_raw = w_stage[:].rearrange("p (c n) -> p c n", c=C)
        mix_raw = w_stage[:].rearrange("p (w c n) -> p w c n", w=4, c=C)
        b_raw = q_t[0:1, 0, 0, 0:D]

        two = ExitStack()
        kv_bd = sb("kv_bd", [P, B, 2, C, P], stack=two)
        diff = sb("diff", [P, C, BLK], stack=two)
        x_mix = sb("x_mix", [P, C, BLK], stack=two)
        xk_hi = sb("xk_hi", [P, C, BLK], F32R, stack=two)
        xk_lo = sb("xk_lo", [P, C, BLK], F32R, stack=two)
        xr_hi = sb("xr_hi", [P, C, BLK], F32R, stack=two)
        q_rot = sb("q_rot", [P, 2, C, BLK], stack=two)
        xr_lo = sb("xr_lo", [P, C, BLK], F32R, stack=two)
        k_relu = sb("k_relu", [P, BLK], stack=two)
        k_sq = sb("k_sq", [P, BLK], stack=two)
        ka_hi = sb("ka_hi", [P, C, BLK], F32R, stack=two)
        ka_lo = sb("ka_lo", [P, C, BLK], F32R, stack=two)
        x_res = sb("x_res", [P, B, T, D], stack=two)
        z = sb("z", [P, T, D], stack=two)
        z_aff = sb("z_aff", [P, C, BLK], stack=two)
        u_in = sb("u_in", [P, C, BLK], stack=two)
        gated = sb("gated", [P, C, BLK], stack=two)
        r_tanh = sb("r_tanh", [P, T, D], stack=two)
        g_hi = sb("g_hi", [P, C, BLK], F32R, stack=two)
        g_lo = sb("g_lo", [P, C, BLK], F32R, stack=two)
        y = sb("y", [P, B, T, D], stack=two)
        two.close()
        u_dram = nc.dram_tensor("u_dram", [B, C, P, N], F32, kind="Internal").ap()

        bank = [ctx.enter_context(nc.psum_tensor(f"bank{i}", [P, BLK], F32)) for i in range(4)]
        pair_a = ctx.enter_context(nc.psum_tensor("pair_a", [P, 2, BLK], F32))
        pair_b = ctx.enter_context(nc.psum_tensor("pair_b", [P, 2, BLK], F32))
        k_ps, v_ps, rot_ps, kv_ps = bank
        xn_ps, qu_ps = pair_a, pair_b
        o_ps, z_ps = pair_a, pair_b
        kf_ps = bank[0]
        vf_ps = bank[1], bank[2]
        r_ps = bank[2], z_ps[:, 0]
        w_ps = bank[3], z_ps[:, 1]

        x_loaded = [sem(f"x_loaded{b}") for b in range(B)]
        w_loaded = [sem("w_kv_loaded"), sem("w_qu_loaded")]
        consts_loaded = sem("consts_loaded")
        small_loaded = sem("small_loaded")
        mix_loaded = sem("mix_loaded")
        bout_loaded = sem("bout_loaded")
        zeroed = sem("zeroed")
        w_hi_ready, w_lo_ready = sem("w_hi_ready"), sem("w_lo_ready")
        dve_step = sem("dve_step")
        pool_step = sem("pool_step")
        stats_ready = sem("stats_ready")
        angle_step = sem("angle_step")
        mix_halved, mix_hi_ready, mix_lo_ready = sem("mix_halved"), sem("mix_hi_ready"), sem("mix_lo_ready")
        b_row_ready = sem("b_row_ready")
        u_spilled = [sem(f"u_spilled{b}") for b in range(B)]
        mv_ready, rstd_ready = sem("mv_ready"), sem("rstd_ready")
        xn_ready = sem("xn_ready")
        xn_transposed = sem("xn_transposed")
        xn_t_ready = sem("xn_t_ready")
        split_ready = sem("split_ready")
        k_proj, v_proj = sem("k_proj"), sem("v_proj")
        k_silu_ready, v_ready = sem("k_silu_ready"), sem("v_ready")
        q_proj, u_proj = sem("q_proj"), sem("u_proj")
        q_ready, u_ready = sem("q_ready"), sem("u_ready")
        k_rot_ready = sem("k_rot_ready")
        kv_done, kv_added = sem("kv_done"), sem("kv_added")
        rot_ready = sem("rot_ready")
        rot_transposed, rot_t_ready = sem("rot_transposed"), sem("rot_t_ready")
        kv_bd_zeroed = sem("kv_bd_zeroed")
        kv_turned, kv_bd_ready = sem("kv_turned"), sem("kv_bd_ready")
        diff_ready = sem("diff_ready")
        xk_raw_ready, xk_split = sem("xk_raw_ready"), sem("xk_split")
        xr_raw_ready, xr_split = sem("xr_raw_ready"), sem("xr_split")
        q_rot_ready = sem("q_rot_ready")
        o_done = sem("o_done")
        mv2_ready, rstd2_ready = sem("mv2_ready"), sem("rstd2_ready")
        z_ready = sem("z_ready")
        z_transposed = sem("z_transposed")
        aff_ready, gated_ready = sem("aff_ready"), sem("gated_ready")
        kf_done, relu_done, k_sq_ready = sem("kf_done"), sem("relu_done"), sem("k_sq_ready")
        ka_hi_ready, ka_lo_ready = sem("ka_hi_ready"), sem("ka_lo_ready")
        g_hi_ready, g_lo_ready = sem("g_hi_ready"), sem("g_lo_ready")
        u_loaded = sem("u_loaded")
        r_done, tanh_ready = sem("r_done"), sem("tanh_ready")
        vf_done, rv_ready = sem("vf_done"), sem("rv_ready")
        w_done, y_ready = sem("w_done"), sem("y_ready")
        res_loaded = [sem(f"res_loaded{b}") for b in range(B)]
        xb_ready, y_part = sem("xb_ready"), sem("y_part")
        stored = [sem(f"stored{b}") for b in range(B)]

        block = ctx.enter_context(nc.Block())

        def turns(eng, body):
            body(0, False)
            with eng.Fori(1, NP - 1) as p:
                body(p, False)
            body(NP - 1, True)

        def wait_for(eng, semaphore, count):
            if not (isinstance(count, int) and count <= 0):
                eng.wait_ge(semaphore, count)

        def unit(p, b):
            return 2 * p + b

        def next_unit(p, b):
            return (p, 1) if b == 0 else (p + 1, 0)

        def unit_before(p, b):
            return (p, 0) if b == 1 else (p - 1, 1)

        def has_before(p, b):
            return not (isinstance(p, int) and p == 0 and b == 0)

        def tokens(p, shift=0):
            return bass.ds(p * BLK + shift, BLK)

        @block.sync
        def _(sp):
            sp.dma_start(x_in[:, 0], x_v[0, 0]).then_inc(x_loaded[0], 16)
            w_v = w_qkvu_t.rearrange("(c p) n -> p c n", p=P)
            sp.dma_start(w_raw[:, :, 0:2 * D], w_v[:, :, 0:2 * D]).then_inc(w_loaded[0], 16)
            sp.dma_start(x_in[:, 1], x_v[1, 0]).then_inc(x_loaded[1], 16)
            sp.dma_start(w_raw[:, :, 2 * D:], w_v[:, :, 2 * D:]).then_inc(w_loaded[1], 16)
            sp.wait_ge(w_hi_ready, 2)
            sp.wait_ge(w_lo_ready, 2)
            for i, w in enumerate((w_r_t, w_k_t, w_v_t, w_out_t)):
                sp.dma_start(mix_raw[:, i], w.rearrange("(c p) n -> p c n", p=P)).then_inc(mix_loaded, 16)

            def phase1(p, last):
                for b in range(B):
                    u = unit(p, b)
                    if not last:
                        sp.wait_ge(xn_transposed, u + 1)
                        sp.dma_start(x_in[:, b], x_v[b, bass.ds(p + 1, 1)].rearrange("o i t c -> i (o t) c")
                                     ).then_inc(x_loaded[b], 16)
                    sp.wait_ge(u_ready, 2 * u + 2)
                    sp.dma_start(u_dram[b, :, :, tokens(p)].rearrange("c p n -> p c n"), u_out[:, b]
                                 ).then_inc(u_spilled[b], 16)

            turns(sp, phase1)
            sp.wait_ge(xn_transposed, B * NP)

            def store(p, b, u):
                sp.wait_ge(y_ready, 2 * u + 2)
                sp.dma_start(out_v[b, bass.ds(p, 1)].rearrange("o i t c -> i (o t) c"), y[:, b]
                             ).then_inc(stored[b], 16)

            def phase2(p, last):
                for b in range(B):
                    u = unit(p, b)
                    wait_for(sp, y_part, 2 * (u - 1))
                    sp.dma_start(x_res[:, b], x_v[b, bass.ds(p, 1)].rearrange("o i t c -> i (o t) c")
                                 ).then_inc(res_loaded[b], 16)
                    if isinstance(p, int) and p == 0:
                        sp.wait_ge(u_spilled[b], 16 * NP)
                        sp.wait_ge(k_rot_ready, 2 * B * NP)
                    wait_for(sp, gated_ready, 2 * u)
                    sp.dma_start(u_in[:], u_dram[b, :, :, tokens(p)].rearrange("c p n -> p c n")
                                 ).then_inc(u_loaded, 16)
                    if has_before(p, b):
                        store(*unit_before(p, b), u - 1)

            turns(sp, phase2)
            store(NP - 1, B - 1, B * NP - 1)
            for b in range(B):
                sp.wait_ge(stored[b], 16 * NP)

        @block.gpsimd
        def _(pool):
            nc.gpsimd.memset(neg_half[:], -0.5).then_inc(pool_step, 1)
            nc.gpsimd.memset(kv_acc[:], 0.0).then_inc(zeroed, 1)
            nc.gpsimd.memset(xn_t[:, :, :, 0:1], 0.0).then_inc(zeroed, 1)
            nc.gpsimd.memset(neg_one[:], -1.0).then_inc(pool_step, 1)
            nc.gpsimd.memset(eps[:], EPS).then_inc(pool_step, 1)
            pool.wait_ge(pool_step, 3)

            def rstd_of(b, ready, base):
                nc.gpsimd.tensor_tensor(rstd[:, b], mv[:, b, :, 1], eps[:], ALU.add).then_inc(pool_step, 1)
                nc.gpsimd.tensor_tensor(nmr[:, b], mv[:, b, :, 0], neg_one[:], ALU.mult).then_inc(pool_step, 1)
                pool.wait_ge(pool_step, base + 2)
                nc.gpsimd.tensor_tensor(rstd[:, b], rstd[:, b], neg_half[:], ALU.pow).then_inc(pool_step, 1)
                pool.wait_ge(pool_step, base + 3)
                nc.gpsimd.tensor_tensor(nmr[:, b], nmr[:, b], rstd[:, b], ALU.mult).then_inc(ready, 1)

            def phase1(p, last):
                for b in range(B):
                    u = unit(p, b)
                    pool.wait_ge(mv_ready, u + 1)
                    rstd_of(b, rstd_ready, 3 + 3 * u)
                    if isinstance(p, int) and p == 0:
                        half = slice(b * 2 * D, (b + 1) * 2 * D)
                        pool.wait_ge(w_hi_ready, b + 1)
                        nc.gpsimd.tensor_tensor(w_lo[:, :, half], w_raw[:, :, half], w_hi[:, :, half].bitcast(F32),
                                                ALU.subtract).then_inc(w_lo_ready, 1)

            turns(pool, phase1)
            pool.wait_ge(rot_ready, 2 * NP)
            nc.gpsimd.memset(kv_bd[:], 0.0).then_inc(kv_bd_zeroed, 1)
            pool.wait_ge(mix_hi_ready, 1)
            nc.gpsimd.tensor_tensor(mix_lo[:], mix_raw, mix_hi[:].bitcast(F32), ALU.subtract).then_inc(mix_lo_ready, 1)
            pool.wait_ge(xn_t_ready, B * NP)

            def make_diff(p, b, u):
                wait_for(pool, xr_raw_ready, u)
                nc.gpsimd.tensor_tensor(diff[:], xn_t[:, :, b, tokens(p, 1)], xn_t[:, :, b, tokens(p)],
                                        ALU.subtract).then_inc(diff_ready, 1)

            def xr_low(u):
                pool.wait_ge(xr_raw_ready, u + 1)
                pool.wait_ge(xr_split, 2 * u + 1)
                nc.gpsimd.tensor_tensor(xr_lo[:], x_mix[:], xr_hi[:].bitcast(F32), ALU.subtract).then_inc(xr_split, 1)

            make_diff(0, 0, 0)
            xr_low(0)
            pool.wait_ge(bout_loaded, 16)

            def add_residual(b, u, j):
                pool.wait_ge(xb_ready, u + 1)
                pool.wait_ge(rv_ready, 2 * u + j + 1)
                nc.gpsimd.tensor_tensor(y[:, b, 2 * j:2 * j + 2], y[:, b, 2 * j:2 * j + 2],
                                        x_res[:, b, 2 * j:2 * j + 2], ALU.add).then_inc(y_part, 1)

            def phase2(p, last):
                for b in range(B):
                    u = unit(p, b)
                    end = last and b == 1
                    if not end:
                        make_diff(*next_unit(p, b), u + 1)
                    if has_before(p, b):
                        add_residual(1 - b, u - 1, 1)
                    pool.wait_ge(mv2_ready, u + 1)
                    rstd_of(b, rstd2_ready, 3 + 3 * B * NP + 3 * u)
                    pool.wait_ge(res_loaded[b], 16 * (p + 1))
                    nc.gpsimd.tensor_tensor(x_res[:, b], x_res[:, b], b_out_bc[:].unsqueeze(1).to_broadcast([P, T, D]),
                                            ALU.add).then_inc(xb_ready, 1)
                    if not end:
                        xr_low(u + 1)
                    add_residual(b, u, 0)

            turns(pool, phase2)
            add_residual(B - 1, B * NP - 1, 1)

        @block.scalar
        def _(act):
            act.dma_start(const[:], consts).then_inc(consts_loaded, 16)
            act.dma_start(theta_bc[:], theta.to_broadcast([P, D])).then_inc(consts_loaded, 16)
            nc.scalar.preload_act_table_set("silu_and_others")
            act.dma_start(b_raw, b_qkvu[:, 0:D]).then_inc(small_loaded, 16)
            act.dma_start(b_v_bc[:], b_qkvu[:, D:2 * D].to_broadcast([P, D])).then_inc(small_loaded, 16)
            col = lambda a: a.rearrange("o (c p) -> p (o c)", p=P)
            with nc.allow_non_contiguous_dma(reason="six columns of a few hundred bytes"):
                for dst, src in ((bq, col(b_qkvu[:, 2 * D:3 * D])), (bu, col(b_qkvu[:, 3 * D:4 * D])),
                                 (lnw, col(ln_w)), (lnb, col(ln_b)), (mur, col(mu_r)), (muk, col(mu_k))):
                    act.dma_start(dst, src).then_inc(small_loaded, 16)
            act.dma_start(b_out_bc[:], b_out.to_broadcast([P, D])).then_inc(bout_loaded, 16)

            def keep_xn_t(p, b, u):
                act.wait_ge(xn_transposed, u + 1)
                nc.scalar.activation(xn_t[:, :, b, tokens(p, 1)], xn_ps[:], ACT.Copy).then_inc(xn_t_ready, 1)

            def sin_cos(n):
                act.wait_ge(angle_step, 7 * (n + 1))
                nc.scalar.activation(rot[:, 1], angle[:, 0], ACT.Sin).then_inc(rot_ready, 1)
                nc.scalar.activation(rot[:, 0], angle[:, 1], ACT.Sin, bias=half_pi[:], scale=-1.0).then_inc(rot_ready, 1)

            def keep_rot_t(p, j, count):
                act.wait_ge(rot_transposed, count + 1)
                nc.scalar.activation(rot_t[:, j // C, j % C, tokens(p)], rot_ps[:], ACT.Copy).then_inc(rot_t_ready, 1)

            for i in range(2):
                act.wait_ge(w_loaded[i], 16)
                half = slice(i * 2 * D, (i + 1) * 2 * D)
                nc.scalar.activation(w_hi[:, :, half], w_raw[:, :, half], ACT.Copy).then_inc(w_hi_ready, 1)
                if i == 0:
                    act.wait_ge(zeroed, 4)
                    keep_xn_t(0, 0, 0)
            act.wait_ge(small_loaded, 16 * SMALL_LOADS)
            act.wait_ge(b_row_ready, 1)

            def phase1(p, last):
                for b in range(B):
                    u = unit(p, b)
                    for j in range(2):
                        act.wait_ge(k_proj, 2 * u + j + 1)
                        if j == 0:
                            wait_for(act, k_rot_ready, 2 * u)
                        nc.scalar.activation(k_silu[:, 2 * j:2 * j + 2], k_ps[:].rearrange("p (t n) -> p t n", t=2),
                                             ACT.Silu).then_inc(k_silu_ready, 1)
                    if isinstance(p, int) and u == 0:
                        sin_cos(0)
                    if not (last and b == 1):
                        keep_xn_t(*next_unit(p, b), u + 1)
                    keep_rot_t(p, 2 * b, 4 * p + 2 * b)
                    for c in range(C):
                        act.wait_ge(q_proj, 2 * u + c + 1)
                        nc.scalar.activation(q_t[:, c, b, tokens(p)], qu_ps[:, c], ACT.Silu, bias=bq[:, c:c + 1]
                                             ).then_inc(q_ready, 1)
                    for c in range(C):
                        act.wait_ge(u_proj, 2 * u + c + 1)
                        wait_for(act, u_spilled[b], 16 * p)
                        nc.scalar.activation(u_out[:, b, c], qu_ps[:, c], ACT.Identity, bias=bu[:, c:c + 1]
                                             ).then_inc(u_ready, 1)
                    keep_rot_t(p, 2 * b + 1, 4 * p + 2 * b + 1)
                    if last and b == 0:
                        act.wait_ge(mix_loaded, 16 * 4)
                        nc.scalar.activation(mix_raw[:, 2], mix_raw[:, 2], ACT.Copy, scale=0.5).then_inc(mix_halved, 1)
                        act.wait_ge(mix_halved, 1)
                        nc.scalar.activation(mix_hi[:], mix_raw, ACT.Copy).then_inc(mix_hi_ready, 1)
                if not last:
                    act.wait_ge(k_rot_ready, 2 * unit(p, 1) + 2)
                    sin_cos(p + 1)

            turns(act, phase1)

            def split_xr(u):
                act.wait_ge(xr_raw_ready, u + 1)
                wait_for(act, r_done, 2 * u)
                nc.scalar.activation(xr_hi[:], x_mix[:], ACT.Copy).then_inc(xr_split, 1)

            def split_xk(u):
                act.wait_ge(xk_raw_ready, u + 1)
                wait_for(act, kf_done, 2 * u)
                nc.scalar.activation(xk_hi[:], x_mix[:], ACT.Copy).then_inc(xk_split, 1)

            def gate(u, j):
                act.wait_ge(r_done, 2 * u + j + 1)
                wait_for(act, rv_ready, 2 * u)
                nc.scalar.activation(r_tanh[:, 2 * j:2 * j + 2], r_ps[j][:].rearrange("p (t n) -> p t n", t=2),
                                     ACT.Tanh, scale=0.5).then_inc(tanh_ready, 1)

            def split_gated(u):
                for c in range(C):
                    act.wait_ge(gated_ready, 2 * u + c + 1)
                    wait_for(act, w_done, 2 * u)
                    nc.scalar.activation(g_hi[:, c], gated[:, c], ACT.Copy).then_inc(g_hi_ready, 1)

            def phase2(p, last):
                for b in range(B):
                    u = unit(p, b)
                    end = last and b == 1
                    for c in range(C):
                        act.wait_ge(kf_done, 2 * u + c + 1)
                        wait_for(act, ka_hi_ready, 2 * u + c)
                        nc.scalar.activation(k_relu[:], kf_ps[:], ACT.Relu).then_inc(relu_done, 1)
                        act.wait_ge(relu_done, 2 * u + c + 1)
                        wait_for(act, ka_lo_ready, 2 * u + c)
                        nc.scalar.activation(k_sq[:], k_relu[:], ACT.Square).then_inc(k_sq_ready, 1)
                        wait_for(act, vf_done, 2 * u)
                        nc.scalar.activation(ka_hi[:, c], k_relu[:], ACT.Square).then_inc(ka_hi_ready, 1)
                        if c == 0 and has_before(p, b):
                            split_gated(u - 1)
                    gate(u, 0)
                    if not end:
                        split_xk(u + 1)
                    act.wait_ge(rstd2_ready, u + 1)
                    wait_for(act, z_transposed, u)
                    for t in range(T):
                        ins = nc.scalar.activation(z[:, t], o_ps[:, t // 2, (t % 2) * D:(t % 2 + 1) * D], ACT.Identity,
                                                   bias=nmr[:, b, t:t + 1], scale=rstd[:, b, t:t + 1])
                    ins.then_inc(z_ready, 1)
                    gate(u, 1)
                    if not end:
                        split_xr(u + 1)
                    for c in range(C):
                        act.wait_ge(z_transposed, u + 1)
                        wait_for(act, gated_ready, 2 * u)
                        nc.scalar.activation(z_aff[:, c], z_ps[:, c], ACT.Identity, bias=lnb[:, c:c + 1],
                                             scale=lnw[:, c:c + 1]).then_inc(aff_ready, 1)

            split_xk(0)
            split_xr(0)
            turns(act, phase2)
            split_gated(B * NP - 1)

        @block.vector
        def _(dve):
            count = [0]

            def then(ins):
                count[0] += 1
                ins.then_inc(dve_step, 1)
                dve.wait_ge(dve_step, count[0])

            nc.vector.memset(half_pi[:], float(np.float32(np.pi / 2))).then_inc(zeroed, 1)
            nc.vector.memset(ones_r[:].bitcast(F32), 1.0).then_inc(zeroed, 1)
            then(nc.vector.memset(b_row[:].bitcast(F32), 0.0))

            def stats1(p, b, u):
                dve.wait_ge(x_loaded[b], 16 * (p + 1))
                for t in range(T):
                    nc.vector.bn_stats(stats[:, t], x_in[:, b, t]).then_inc(stats_ready, 1)
                dve.wait_ge(stats_ready, T * (u + 1))
                nc.vector.memset(tick[:], 0.0)
                for t in range(T):
                    ins = nc.vector.bn_aggr(mv[:, b, t], stats[:, t])
                ins.then_inc(mv_ready, 1)

            def norm1(b, u):
                dve.wait_ge(rstd_ready, u + 1)
                for t in range(T):
                    ins = nc.vector.tensor_scalar(x_in[:, b, t], x_in[:, b, t], mv[:, b, t, 0:1], rstd[:, b, t:t + 1],
                                                  ALU.subtract, ALU.mult)
                ins.then_inc(xn_ready, 1)

            def split(p, b, u):
                dve.wait_ge(xn_t_ready, u + 1)
                wait_for(dve, u_proj, 2 * (u - 1))
                nc.vector.tensor_copy(xn_hi[:, b], xn_t[:, :, b, tokens(p, 1)]).then_inc(split_ready, 1)
                dve.wait_ge(split_ready, 2 * u + 1)
                nc.vector.tensor_tensor(xn_lo[:, b], xn_t[:, :, b, tokens(p, 1)], xn_hi[:, b].bitcast(F32),
                                        ALU.subtract).then_inc(split_ready, 1)

            ANGLE_STEPS = 7

            def angles(n, first, end):
                a, k = angle[:, 0], angle[:, 1]
                steps = (
                    lambda: nc.vector.tensor_tensor(a, theta_bc[:].unsqueeze(1).to_broadcast([P, T, D]),
                                                    pos[:, bass.ds(n * T, T)].unsqueeze(2).to_broadcast([P, T, D]),
                                                    ALU.mult),
                    lambda: nc.vector.tensor_scalar(k, a, INV_TWO_PI, ROUND, ALU.mult, ALU.add),
                    lambda: nc.vector.tensor_scalar(k, k, -ROUND, None, ALU.add),
                    lambda: nc.vector.scalar_tensor_tensor(a, k, -TWO_PI_HI, a, ALU.mult, ALU.add),
                    lambda: nc.vector.scalar_tensor_tensor(a, k, -TWO_PI_LO, a, ALU.mult, ALU.add),
                    lambda: nc.vector.tensor_scalar(a, a, PI_BELOW, -PI_BELOW, ALU.min, ALU.max),
                    lambda: nc.vector.tensor_scalar(k.bitcast(U32), a.bitcast(U32), 0x7FFFFFFF, None, ALU.bitwise_and),
                )
                assert len(steps) == ANGLE_STEPS
                for i in range(first, end):
                    if i == 0:
                        wait_for(dve, rot_ready, 2 * n)
                    else:
                        dve.wait_ge(angle_step, ANGLE_STEPS * n + i)
                    steps[i]().then_inc(angle_step, 1)

            def rotate_k(u, j, b):
                dve.wait_ge(k_silu_ready, 2 * u + j + 1)
                if j == 0:
                    wait_for(dve, kv_done, u)
                for cs in range(2):
                    ins = nc.vector.tensor_tensor(k_rot[:, 2 * j:2 * j + 2, cs], k_silu[:, 2 * j:2 * j + 2],
                                                  rot[:, cs, 2 * j:2 * j + 2], ALU.mult)
                ins.then_inc(k_rot_ready, 1)

            def add_kv(b, u):
                dve.wait_ge(kv_done, u + 1)
                nc.vector.tensor_tensor(kv_acc[:, b], kv_acc[:, b],
                                        kv_ps[:, 0:C * 2 * G].rearrange("p (c s g) -> p c s g", c=C, s=2),
                                        ALU.add).then_inc(kv_added, 1)

            def add_bias_v(u, j):
                dve.wait_ge(v_proj, 2 * u + j + 1)
                wait_for(dve, kv_done, u)
                nc.vector.tensor_tensor(v_sb[:, 2 * j:2 * j + 2], v_ps[:].rearrange("p (t n) -> p t n", t=2),
                                        b_v_bc[:].unsqueeze(1).to_broadcast([P, 2, D]), ALU.add).then_inc(v_ready, 1)

            dve.wait_ge(consts_loaded, 32)
            angles(0, 0, 3)
            stats1(0, 0, 0)
            angles(0, 3, 4)
            norm1(0, 0)
            angles(0, 4, 5)
            dve.wait_ge(small_loaded, 16 * SMALL_LOADS)
            then(nc.vector.tensor_copy(b_row[0:1], b_raw))
            nc.vector.tensor_tensor(b_row[32:33], b_raw, b_row[0:1].bitcast(F32), ALU.subtract).then_inc(b_row_ready, 1)
            dve.wait_ge(zeroed, 4)
            split(0, 0, 0)
            stats1(0, 1, 1)
            angles(0, 5, ANGLE_STEPS)

            def phase1(p, last):
                for b in range(B):
                    u = unit(p, b)
                    end = last and b == 1
                    if not end:
                        norm1(next_unit(p, b)[1], u + 1)
                    for j in range(2):
                        if b == 0 and j == 0:
                            if isinstance(p, int) and p == 0:
                                add_bias_v(u, 0)
                                add_bias_v(u, 1)
                            dve.wait_ge(rot_ready, 2 * p + 2)
                        rotate_k(u, j, b)
                        if not (isinstance(p, int) and u == 0):
                            add_bias_v(u, j)
                    if not end:
                        split(*next_unit(p, b), u + 1)
                    if not last:
                        stats1(p + 1, b, u + 2)
                        angles(p + 1, *((0, 4) if b == 0 else (4, ANGLE_STEPS)))
                    if end:
                        dve.wait_ge(kv_bd_zeroed, 1)
                        block_diagonal(0, xn_ps[:, 0])
                        xk_raw(0, 0, 0)
                        dve.wait_ge(u_proj, 2 * B * NP)
                        dve.wait_ge(rot_t_ready, 4 * (NP - 1))
                        rotate_q(0, 0, 0, 0, 1)
                        xk_low(0)
                    add_kv(b, u)

            def block_diagonal(b, turned):
                dve.wait_ge(kv_turned, b + 1)
                turned = turned[:, 0:C * P].rearrange("p (c e) -> p c e", c=C)
                for cs in range(2):
                    for h in range(2):
                        rows, src, e = slice(G * h, G * h + G), slice(G * cs, G * cs + G), slice(G * h, G * h + G)
                        ins = nc.vector.tensor_tensor(kv_bd[rows, b, cs, :, e], turned[src, :, e],
                                                      mask[src].unsqueeze(1).to_broadcast([G, C, G]), ALU.mult)
                ins.then_inc(kv_bd_ready, 1)

            def rotate_q(p, b, u, *parts):
                wait_for(dve, o_done, 2 * u)
                for cs in parts:
                    nc.vector.tensor_tensor(q_rot[:, cs], q_t[:, :, b, tokens(p)], rot_t[:, cs, :, tokens(p)],
                                            ALU.mult).then_inc(q_rot_ready, 1)

            def mixed(mu, p, b, u, ready):
                dve.wait_ge(diff_ready, u + 1)
                for c in range(C):
                    ins = nc.vector.scalar_tensor_tensor(x_mix[:, c], diff[:, c], mu[:, c:c + 1],
                                                         xn_t[:, c, b, tokens(p)], ALU.mult, ALU.add)
                ins.then_inc(ready, 1)

            def xk_raw(p, b, u):
                wait_for(dve, xr_split, 2 * u)
                mixed(muk, p, b, u, xk_raw_ready)

            def xk_low(u):
                dve.wait_ge(xk_split, 2 * u + 1)
                nc.vector.tensor_tensor(xk_lo[:], x_mix[:], xk_hi[:].bitcast(F32), ALU.subtract).then_inc(xk_split, 1)

            def xr_raw(p, b, u):
                dve.wait_ge(xk_split, 2 * u + 2)
                mixed(mur, p, b, u, xr_raw_ready)

            def ka_low(u, c):
                dve.wait_ge(k_sq_ready, 2 * u + c + 1)
                dve.wait_ge(ka_hi_ready, 2 * u + c + 1)
                nc.vector.tensor_tensor(ka_lo[:, c], k_sq[:], ka_hi[:, c].bitcast(F32), ALU.subtract
                                        ).then_inc(ka_lo_ready, 1)

            def gated_low(u):
                dve.wait_ge(g_hi_ready, 2 * u + 2)
                nc.vector.tensor_tensor(g_lo[:], gated[:], g_hi[:].bitcast(F32), ALU.subtract).then_inc(g_lo_ready, 1)

            def finish(p, b, u, j):
                dve.wait_ge(w_done, 2 * u + j + 1)
                dve.wait_ge(y_part, 2 * u + j + 1)
                nc.vector.tensor_tensor(y[:, b, 2 * j:2 * j + 2], w_ps[j][:].rearrange("p (t n) -> p t n", t=2),
                                        y[:, b, 2 * j:2 * j + 2], ALU.add).then_inc(y_ready, 1)

            turns(dve, phase1)
            xr_raw(0, 0, 0)

            def phase2(p, last):
                for b in range(B):
                    u = unit(p, b)
                    end = last and b == 1

                    def gate_v(j):
                        dve.wait_ge(vf_done, 2 * u + j + 1)
                        dve.wait_ge(tanh_ready, 2 * u + j + 1)
                        if isinstance(p, int) and u == 0 and j == 0:
                            for spilled in u_spilled:
                                dve.wait_ge(spilled, 16 * NP)
                        if j == 0:
                            wait_for(dve, stored[b], 16 * p)
                        nc.vector.scalar_tensor_tensor(y[:, b, 2 * j:2 * j + 2], r_tanh[:, 2 * j:2 * j + 2], 1.0,
                                                       vf_ps[j][:].rearrange("p (t n) -> p t n", t=2),
                                                       ALU.add, ALU.mult).then_inc(rv_ready, 1)

                    for j in range(2):
                        if j == 0:
                            ka_low(u, 0)
                        dve.wait_ge(o_done, 2 * u + j + 1)
                        for i in range(2):
                            nc.vector.bn_stats(stats[:, 2 * j + i], o_ps[:, j, i * D:(i + 1) * D]).then_inc(stats_ready, 1)
                        if j == 0 and has_before(p, b):
                            gated_low(u - 1)
                    dve.wait_ge(stats_ready, T * (B * NP + u + 1))
                    nc.vector.memset(tick[:], 0.0)
                    for t in range(T):
                        ins = nc.vector.bn_aggr(mv[:, b, t], stats[:, t])
                    ins.then_inc(mv2_ready, 1)
                    ka_low(u, 1)
                    if isinstance(p, int) and p == 0 and b == 0:
                        dve.wait_ge(rot_t_ready, 4 * NP)
                        block_diagonal(1, w_ps[0])
                    if not end:
                        xk_raw(*next_unit(p, b), u + 1)
                        rotate_q(*next_unit(p, b), u + 1, 0)
                    if has_before(p, b):
                        finish(*unit_before(p, b), u - 1, 0)
                    if not end:
                        xk_low(u + 1)
                    if has_before(p, b):
                        finish(*unit_before(p, b), u - 1, 1)
                    if not end:
                        xr_raw(*next_unit(p, b), u + 1)
                        rotate_q(*next_unit(p, b), u + 1, 1)
                    gate_v(0)
                    gate_v(1)
                    for c in range(C):
                        dve.wait_ge(aff_ready, 2 * u + c + 1)
                        if c == 0:
                            dve.wait_ge(u_loaded, 16 * (u + 1))
                            wait_for(dve, g_lo_ready, u)
                        nc.vector.tensor_tensor(gated[:, c], z_aff[:, c], u_in[:, c], ALU.mult).then_inc(gated_ready, 1)

            turns(dve, phase2)
            gated_low(B * NP - 1)
            for j in range(2):
                finish(NP - 1, B - 1, B * NP - 1, j)

        @block.tensor
        def _(pe):
            K0, V0, Q0, U0 = 0, D, 2 * D, 3 * D

            def turn_xn(b, u):
                pe.wait_ge(xn_ready, u + 1)
                wait_for(pe, xn_t_ready, u)
                for c in range(C):
                    for t in range(T):
                        ins = nc.tensor.transpose(xn_ps[:, c, t * P:(t + 1) * P], x_in[:, b, t, c * P:(c + 1) * P], ident)
                ins.then_inc(xn_transposed, 1)

            def tile_pair(ps, b, j, w0, bias):
                if bias:
                    nc.tensor.matmul(ps[:], ones_r[:], b_row[:].unsqueeze(1).to_broadcast([P, 2, D]),
                                     start=True, stop=False)
                for i in range(2):
                    t = 2 * j + i
                    for c in range(C):
                        for x_part, w_part in ((xn_hi, w_hi), (xn_hi, w_lo), (xn_lo, w_hi)):
                            ins = nc.tensor.matmul(ps[:, i * D:(i + 1) * D], x_part[:, b, c, t * P:(t + 1) * P],
                                                   w_part[:, c, w0:w0 + D],
                                                   start=not bias and c == 0 and x_part is xn_hi and w_part is w_hi,
                                                   stop=(i == 1 or not bias) and c == C - 1 and x_part is xn_lo)
                return ins

            def channels(ps, b, w0):
                for c in range(C):
                    for w_part, x_part in ((w_hi, xn_hi), (w_lo, xn_hi), (w_hi, xn_lo)):
                        ins = nc.tensor.matmul(ps, w_part[:, c, w0:w0 + P], x_part[:, b, c],
                                               start=c == 0 and w_part is w_hi and x_part is xn_hi,
                                               stop=c == C - 1 and x_part is xn_lo)
                return ins

            def turn_kv(b, ps):
                pe.wait_ge(kv_added, 2 * NP - 1 + b)
                for c in range(C):
                    ins = nc.tensor.transpose(ps[:, c * P:(c + 1) * P],
                                              kv_acc[:, b, c].rearrange("p s g -> p (s g)"), ident)
                ins.then_inc(kv_turned, 1)

            def turn_rot(j, count):
                wait_for(pe, rot_t_ready, count)
                for t in range(T):
                    ins = nc.tensor.transpose(rot_ps[:, t * P:(t + 1) * P],
                                              rot[:, j // C, t, (j % C) * P:(j % C + 1) * P], ident)
                ins.then_inc(rot_transposed, 1)

            pe.wait_ge(consts_loaded, 32)
            turn_xn(0, 0)
            pe.wait_ge(zeroed, 4)
            pe.wait_ge(w_hi_ready, 1)
            pe.wait_ge(w_lo_ready, 1)
            pe.wait_ge(b_row_ready, 1)

            def phase1(p, last):
                for b in range(B):
                    u = unit(p, b)
                    pe.wait_ge(split_ready, 2 * u + 2)
                    for j in range(2):
                        wait_for(pe, k_silu_ready, 2 * u + j)
                        tile_pair(k_ps, b, j, K0, True).then_inc(k_proj, 1)
                        wait_for(pe, v_ready, 2 * u + j)
                        tile_pair(v_ps, b, j, V0, False).then_inc(v_proj, 1)
                    if not (last and b == 1):
                        turn_xn(next_unit(p, b)[1], u + 1)
                    else:
                        pe.wait_ge(xn_t_ready, B * NP)
                        turn_kv(0, xn_ps[:, 0])
                    if b == 0:
                        pe.wait_ge(rot_ready, 2 * p + 2)
                    turn_rot(2 * b, 4 * p + 2 * b)
                    pe.wait_ge(w_hi_ready, 2)
                    pe.wait_ge(w_lo_ready, 2)
                    for c in range(C):
                        wait_for(pe, u_ready, 2 * u)
                        channels(qu_ps[:, c], b, Q0 + c * P).then_inc(q_proj, 1)
                    for c in range(C):
                        pe.wait_ge(q_ready, 2 * u + c + 1)
                        channels(qu_ps[:, c], b, U0 + c * P).then_inc(u_proj, 1)
                    turn_rot(2 * b + 1, 4 * p + 2 * b + 1)
                    pe.wait_ge(v_ready, 2 * u + 2)
                    pe.wait_ge(k_rot_ready, 2 * u + 2)
                    wait_for(pe, kv_added, u)
                    for t in range(T):
                        for c in range(C):
                            for h in range(2):
                                d0 = c * P + h * G
                                ins = nc.tensor.matmul(
                                    kv_ps[h * G:(h + 1) * G, c * 2 * G:(c + 1) * 2 * G],
                                    v_sb[:, t, d0:d0 + G], k_rot[:, t, :, d0:d0 + G],
                                    start=t == 0 and c == 0, stop=t == T - 1, skip_group_check=True)
                    ins.then_inc(kv_done, 1)

            turns(pe, phase1)

            W_R, W_K, W_V, W_O = range(4)

            def rows(ps, x_hi, x_lo, w, j):
                for i in range(2):
                    t = 2 * j + i
                    for c in range(C):
                        for x_part, w_part in ((x_hi, mix_hi), (x_hi, mix_lo), (x_lo, mix_hi)):
                            ins = nc.tensor.matmul(ps[:, i * D:(i + 1) * D], x_part[:, c, t * P:(t + 1) * P],
                                                   w_part[:, w, c],
                                                   start=c == 0 and x_part is x_hi and w_part is mix_hi,
                                                   stop=c == C - 1 and x_part is x_lo)
                return ins

            pe.wait_ge(mix_hi_ready, 1)
            pe.wait_ge(mix_lo_ready, 1)

            def project(u, j):
                pe.wait_ge(g_hi_ready, 2 * u + 2)
                pe.wait_ge(g_lo_ready, u + 1)
                wait_for(pe, y_ready, 2 * u)
                rows(w_ps[j], g_hi, g_lo, W_O, j).then_inc(w_done, 1)

            def phase2(p, last):
                for b in range(B):
                    u = unit(p, b)

                    def attend(j):
                        for i in range(2):
                            t = 2 * j + i
                            for c in range(C):
                                for cs in range(2):
                                    ins = nc.tensor.matmul(o_ps[:, j, i * D + c * P:i * D + (c + 1) * P],
                                                           q_rot[:, cs, c, t * P:(t + 1) * P], kv_bd[:, b, cs, c],
                                                           start=cs == 0, stop=cs == 1)
                        ins.then_inc(o_done, 1)

                    def mix_k(o):
                        wait_for(pe, relu_done, 2 * u + o)
                        for c in range(C):
                            for w_part, x_part in ((mix_hi, xk_hi), (mix_lo, xk_hi), (mix_hi, xk_lo)):
                                ins = nc.tensor.matmul(kf_ps[:], w_part[:, W_K, c, o * P:(o + 1) * P], x_part[:, c],
                                                       start=c == 0 and w_part is mix_hi and x_part is xk_hi,
                                                       stop=c == C - 1 and x_part is xk_lo)
                        ins.then_inc(kf_done, 1)

                    def mix_r(j):
                        wait_for(pe, rv_ready, 2 * u)
                        if j == 1:
                            wait_for(pe, aff_ready, 2 * u)
                        rows(r_ps[j], xr_hi, xr_lo, W_R, j).then_inc(r_done, 1)

                    def mix_v(j):
                        if j == 0:
                            wait_for(pe, rv_ready, 2 * u)
                        else:
                            pe.wait_ge(tanh_ready, 2 * u + 1)
                        rows(vf_ps[j], ka_hi, ka_lo, W_V, j).then_inc(vf_done, 1)

                    pe.wait_ge(xk_split, 2 * u + 2)
                    mix_k(0)
                    if isinstance(p, int) and p == 0:
                        pe.wait_ge(kv_bd_ready, b + 1)
                    pe.wait_ge(q_rot_ready, 2 * u + 2)
                    wait_for(pe, z_ready, u)
                    attend(0)
                    mix_k(1)
                    attend(1)
                    if isinstance(p, int) and p == 0 and b == 0:
                        turn_kv(1, w_ps[0])
                    pe.wait_ge(xr_split, 2 * u + 2)
                    for j in range(2):
                        mix_r(j)
                        if has_before(p, b):
                            project(u - 1, j)
                    pe.wait_ge(ka_hi_ready, 2 * u + 2)
                    pe.wait_ge(ka_lo_ready, 2 * u + 2)
                    mix_v(0)
                    mix_v(1)
                    pe.wait_ge(z_ready, u + 1)
                    for c in range(C):
                        if c == 0:
                            pe.wait_ge(tanh_ready, 2 * u + 2)
                        else:
                            wait_for(pe, y_ready, 2 * u)
                        for t in range(T):
                            ins = nc.tensor.transpose(z_ps[:, c, t * P:(t + 1) * P], z[:, t, c * P:(c + 1) * P], ident)
                    ins.then_inc(z_transposed, 1)

            turns(pe, phase2)
            for j in range(2):
                project(B * NP - 1, j)


def kernel(L0_attn_x, L0_attn_context, L0_attn_Wqkvu, L0_attn_bqkvu, L0_attn_Wout, L0_attn_bout, L0_attn_theta,
           L0_attn_ln_w, L0_attn_ln_b, L0_ffn_W_r, L0_ffn_W_k, L0_ffn_W_v, L0_ffn_mu_r, L0_ffn_mu_k):
    import concourse.bacc as bacc
    from concourse.bass_utils import run_bass_kernel_spmd

    x = np.ascontiguousarray(L0_attn_x)
    d = x.shape[2]
    order = [1, 2, 0, 3]
    w = np.asarray(L0_attn_Wqkvu).reshape(4, d, d)
    bias = np.asarray(L0_attn_bqkvu).reshape(4, d)
    n_tiles = x.shape[1] // P
    p_i = np.arange(P)[:, None]
    identity = (p_i == np.arange(P)[None, :]).astype(np.float32)
    mask = (p_i % 64 // 16 == np.arange(64)[None, :] // 16).astype(np.float32)
    positions = (p_i + P * np.arange(n_tiles)[None, :]).astype(np.float32)
    row = lambda a: np.ascontiguousarray(np.asarray(a).reshape(1, -1))
    arrays = {
        "x": x,
        "w_qkvu_t": np.ascontiguousarray(np.stack([w[i] for i in order]).reshape(4 * d, d).T),
        "b_qkvu": row(np.stack([bias[i] for i in order])),
        "w_out_t": np.ascontiguousarray(np.asarray(L0_attn_Wout).T),
        "b_out": row(L0_attn_bout),
        "theta": row(L0_attn_theta),
        "ln_w": row(L0_attn_ln_w),
        "ln_b": row(L0_attn_ln_b),
        "w_r_t": np.ascontiguousarray(np.asarray(L0_ffn_W_r).T),
        "w_k_t": np.ascontiguousarray(np.asarray(L0_ffn_W_k).T),
        "w_v_t": np.ascontiguousarray(np.asarray(L0_ffn_W_v).T),
        "mu_r": row(L0_ffn_mu_r),
        "mu_k": row(L0_ffn_mu_k),
        "consts": np.concatenate([identity, mask, positions], axis=1),
    }
    nc = bacc.Bacc("TRN2", target_bir_lowering=False, num_devices=1)
    args = [nc.dram_tensor(n, a.shape, mybir.dt.from_np(a.dtype), kind="ExternalInput").ap() for n, a in arrays.items()]
    out = nc.dram_tensor("out", x.shape, mybir.dt.from_np(x.dtype), kind="ExternalOutput").ap()
    lrpe_block_kernel(nc, *args, out)
    result = run_bass_kernel_spmd(nc, [arrays], core_ids=[0])
    return result.results[0]["out"]
```

```python
from contextlib import ExitStack

import concourse.bass as bass
import numpy as np
from concourse import mybir

F32 = mybir.dt.float32
F32R = mybir.dt.float32r
U32 = mybir.dt.uint32
ALU = mybir.AluOpType
ACT = mybir.ActivationFunctionType

P = 128
EPS = 1e-5
TWO_PI_HI = 6.28125
TWO_PI_LO = float(np.float32(2 * np.pi - 6.28125))
INV_TWO_PI = float(np.float32(1 / (2 * np.pi)))
ROUND = float(1.5 * 2**23)
PI_BELOW = 3.1415925


def lrpe_block_kernel(nc, x, w_qkvu_t, b_qkvu, w_out_t, b_out, theta, ln_w, ln_b,
                      w_r_t, w_k_t, w_v_t, mu_r, mu_k, consts, out):
    B, N, D = x.shape
    C = D // P
    BLK = 512
    T = BLK // P
    NP = N // BLK
    NT = N // P
    G = 64
    PARTS = 2 * C
    ANGLE_STEPS = 7
    SMALL_LOADS = 8
    assert B == 2 and D == 2 * P and T == 4

    x_v = x.rearrange("b (p t i) c -> b p i t c", t=T, i=P)
    out_v = out.rearrange("b (p t i) c -> b p i t c", t=T, i=P)

    with ExitStack() as ctx:
        def sb(name, shape, dt=F32, stack=None):
            return (stack or ctx).enter_context(nc.sbuf_tensor(name, shape, dt))

        def sem(name):
            return ctx.enter_context(nc.semaphore(name))

        xn_t = sb("xn_t", [P, C, B, 1 + N])
        q_rot = sb("q_rot", [P, PARTS, B, N])
        mix_hi = sb("mix_hi", [P, 4, C, D], F32R)
        mix_lo = sb("mix_lo", [P, 4, C, D], F32R)
        const = sb("const", [P, P + G + NT])
        cols = sb("cols", [P, 6 * C])
        b_out_bc = sb("b_out_bc", [P, D])
        kv_acc = sb("kv_acc", [P, B, C, 2, G])
        neg_half = sb("neg_half", [P, T])
        neg_one = sb("neg_one", [P, T])
        eps = sb("eps", [P, T])
        half_pi = sb("half_pi", [P, 1])
        tick = sb("tick", [P, 1])
        pool_tick = sb("pool_tick", [P, 1])
        stats = sb("stats", [P, T, 6])
        mv = sb("mv", [P, 2, T, 2])
        rstd = sb("rstd", [P, 2, T])
        nmr = sb("nmr", [P, 2, T])
        ident, mask, pos = const[:, 0:P], const[:, P:P + G], const[:, P + G:P + G + NT]
        bq, bu, lnw, lnb, mur, muk = (cols[:, C * i:C * i + C] for i in range(6))

        one = ExitStack()
        angle = sb("angle", [P, 2, T, D], stack=one)
        w_hi = sb("w_hi", [P, C, 4 * D], F32R, stack=one)
        w_lo = sb("w_lo", [P, C, 4 * D], F32R, stack=one)
        xn_hi = sb("xn_hi", [P, B, C, BLK], F32R, stack=one)
        xn_lo = sb("xn_lo", [P, B, C, BLK], F32R, stack=one)
        x_in = sb("x_in", [P, B, T, D], stack=one)
        rot = sb("rot", [P, 2, T, D], stack=one)
        k_sb = sb("k_sb", [P, T, D], stack=one)
        k_rot = sb("k_rot", [P, T, 2, D], stack=one)
        v_sb = sb("v_sb", [P, T, D], stack=one)
        u_out = sb("u_out", [P, B, C, BLK], stack=one)
        rot_t = sb("rot_t", [P, PARTS, BLK], stack=one)
        theta_bc = sb("theta_bc", [P, D], stack=one)
        b_k_bc = sb("b_k_bc", [P, D], stack=one)
        b_v_bc = sb("b_v_bc", [P, D], stack=one)
        one.close()
        stage = q_rot[:, :, B - 1, N - BLK:]
        w_raw = stage.rearrange("p (c h) n -> p h c n", c=C)
        mix_raw = stage.rearrange("p w (c n) -> p w c n", c=C)

        two = ExitStack()
        kv_bd = sb("kv_bd", [P, B, 2, C, P], stack=two)
        diff = sb("diff", [P, C, BLK], stack=two)
        xk_lo = sb("xk_lo", [P, C, BLK], F32R, stack=two)
        xr_hi = sb("xr_hi", [P, C, BLK], F32R, stack=two)
        x_res = sb("x_res", [P, B, T, D], stack=two)
        xr_lo = sb("xr_lo", [P, C, BLK], F32R, stack=two)
        ka_hi = sb("ka_hi", [P, C, BLK], F32R, stack=two)
        ka_lo = sb("ka_lo", [P, C, BLK], F32R, stack=two)
        z = sb("z", [P, T, D], stack=two)
        x_mix = sb("x_mix", [P, C, BLK], stack=two)
        xk_hi = sb("xk_hi", [P, C, BLK], F32R, stack=two)
        q_in = sb("q_in", [P, B, PARTS, BLK], stack=two)
        gated = sb("gated", [P, C, BLK], stack=two)
        u_in = sb("u_in", [P, C, BLK], stack=two)
        g_hi = sb("g_hi", [P, C, BLK], F32R, stack=two)
        g_lo = sb("g_lo", [P, C, BLK], F32R, stack=two)
        y = sb("y", [P, B, T, D], stack=two)
        k_act = sb("k_act", [P, BLK], stack=two)
        two.close()
        u_dram = nc.dram_tensor("u_dram", [B, C, P, N], F32, kind="Internal").ap()

        bank = [ctx.enter_context(nc.psum_tensor(f"bank{i}", [P, BLK], F32)) for i in range(4)]
        pair_a = ctx.enter_context(nc.psum_tensor("pair_a", [P, 2, BLK], F32))
        pair_b = ctx.enter_context(nc.psum_tensor("pair_b", [P, 2, BLK], F32))
        k_ps, v_ps, rot_ps, kv_ps = bank
        xn_ps, q_ps = pair_a, pair_b
        u_ps = pair_a
        o_ps, z_ps = pair_a, pair_b
        kf_ps = bank[0]
        vf_ps = bank[1], bank[2]
        r_ps = bank[2], z_ps[:, 0]
        w_ps = bank[3], z_ps[:, 1]

        x_loaded = [sem(f"x_loaded{b}") for b in range(B)]
        w_loaded = [sem("w_kv_loaded"), sem("w_qu_loaded")]
        consts_loaded = sem("consts_loaded")
        small_loaded = sem("small_loaded")
        mix_loaded = sem("mix_loaded")
        bout_loaded = sem("bout_loaded")
        zeroed = sem("zeroed")
        half_turned, half_kept, half_split = sem("half_turned"), sem("half_kept"), sem("half_split")
        w_hi_ready, w_lo_ready = sem("w_hi_ready"), sem("w_lo_ready")
        pool_step = sem("pool_step")
        stats_ready = sem("stats_ready")
        angle_step = sem("angle_step")
        mix_halved, mix_hi_ready, mix_lo_ready = sem("mix_halved"), sem("mix_hi_ready"), sem("mix_lo_ready")
        u_spilled = [sem(f"u_spilled{b}") for b in range(B)]
        mv_ready, rstd_ready = sem("mv_ready"), sem("rstd_ready")
        xn_ready = sem("xn_ready")
        xn_transposed = sem("xn_transposed")
        xn_t_ready = sem("xn_t_ready")
        split_ready = sem("split_ready")
        k_proj, v_proj = sem("k_proj"), sem("v_proj")
        k_biased, k_silu_ready = sem("k_biased"), sem("k_silu_ready")
        v_raw, v_ready = sem("v_raw"), sem("v_ready")
        q_proj, u_proj = sem("q_proj"), sem("u_proj")
        q_ready, u_ready = sem("q_ready"), sem("u_ready")
        k_rot_ready = sem("k_rot_ready")
        kv_done, kv_added = sem("kv_done"), sem("kv_added")
        rot_ready = sem("rot_ready")
        rot_transposed, rot_t_ready = sem("rot_transposed"), sem("rot_t_ready")
        kv_turned, kv_bd_ready = sem("kv_turned"), sem("kv_bd_ready")
        diff_ready = sem("diff_ready")
        xk_raw_ready, xk_split = sem("xk_raw_ready"), sem("xk_split")
        xr_raw_ready, xr_split = sem("xr_raw_ready"), sem("xr_split")
        kv_bd_zeroed = sem("kv_bd_zeroed")
        q_rot_ready = sem("q_rot_ready")
        q_loaded = [sem(f"q_loaded{b}") for b in range(B)]
        o_done = sem("o_done")
        mv2_ready, rstd2_ready = sem("mv2_ready"), sem("rstd2_ready")
        z_ready = sem("z_ready")
        z_transposed = sem("z_transposed")
        aff_ready, gated_ready = sem("aff_ready"), sem("gated_ready")
        kf_done, relu_done, k_sq_ready = sem("kf_done"), sem("relu_done"), sem("k_sq_ready")
        ka_hi_ready, ka_lo_ready = sem("ka_hi_ready"), sem("ka_lo_ready")
        g_hi_ready, g_lo_ready = sem("g_hi_ready"), sem("g_lo_ready")
        u_loaded = sem("u_loaded")
        r_done, tanh_ready = sem("r_done"), sem("tanh_ready")
        vf_done, rv_ready = sem("vf_done"), sem("rv_ready")
        w_done, y_ready = sem("w_done"), sem("y_ready")
        res_loaded = [sem(f"res_loaded{b}") for b in range(B)]
        xb_ready, y_part = sem("xb_ready"), sem("y_part")
        stored = [sem(f"stored{b}") for b in range(B)]

        block = ctx.enter_context(nc.Block())

        def turns(eng, body):
            body(0, False)
            with eng.Fori(1, NP - 1) as p:
                body(p, False)
            body(NP - 1, True)

        def wait_for(eng, semaphore, count):
            if not (isinstance(count, int) and count <= 0):
                eng.wait_ge(semaphore, count)

        def is_first(n):
            return isinstance(n, int) and n == 0

        def unit(p, b):
            return 2 * p + b

        def attention_first(p, b):
            return isinstance(p, int) and (p, b) in ((0, 0), (NP - 1, B - 1))

        def next_unit(p, b):
            return (p, 1) if b == 0 else (p + 1, 0)

        def unit_before(p, b):
            return (p, 0) if b == 1 else (p - 1, 1)

        def has_before(p, b):
            return not (is_first(p) and b == 0)

        def tokens(p, shift=0):
            return bass.ds(p * BLK + shift, BLK)

        @block.sync
        def _(sp):
            sp.dma_start(x_in[:, 0], x_v[0, 0]).then_inc(x_loaded[0], 16)
            w_v = w_qkvu_t.rearrange("(c p) n -> p c n", p=P)
            sp.dma_start(w_raw[:, 0], w_v[:, :, 0:2 * D]).then_inc(w_loaded[0], 16)
            sp.dma_start(x_in[:, 1], x_v[1, 0]).then_inc(x_loaded[1], 16)
            sp.dma_start(w_raw[:, 1], w_v[:, :, 2 * D:]).then_inc(w_loaded[1], 16)
            sp.wait_ge(w_hi_ready, 2)
            sp.wait_ge(w_lo_ready, 3)
            for i, w in enumerate((w_r_t, w_k_t, w_v_t, w_out_t)):
                sp.dma_start(mix_raw[:, i], w.rearrange("(c p) n -> p c n", p=P)).then_inc(mix_loaded, 16)

            def load_q(p, b, u):
                wait_for(sp, o_done, 2 * (u - 1))
                sp.dma_start(q_in[:, b], q_rot[:, :, b, tokens(p)]).then_inc(q_loaded[b], 16)

            def phase1(p, last):
                for b in range(B):
                    u = unit(p, b)
                    if not last:
                        sp.wait_ge(xn_transposed, u + 1)
                        sp.dma_start(x_in[:, b], x_v[b, bass.ds(p + 1, 1)].rearrange("o i t c -> i (o t) c")
                                     ).then_inc(x_loaded[b], 16)
                    elif b == 1:
                        sp.wait_ge(k_rot_ready, 2 * B * NP)
                        sp.wait_ge(rot_transposed, 4 * NP)
                        load_q(0, 0, 0)
                    sp.wait_ge(u_ready, 2 * u + 2)
                    sp.dma_start(u_dram[b, :, :, tokens(p)].rearrange("c p n -> p c n"), u_out[:, b]
                                 ).then_inc(u_spilled[b], 16)

            turns(sp, phase1)

            def load_x(p, b, u):
                wait_for(sp, y_part, 2 * (u - 1))
                sp.dma_start(x_res[:, b], x_v[b, bass.ds(p, 1)].rearrange("o i t c -> i (o t) c")
                             ).then_inc(res_loaded[b], 16)

            sp.wait_ge(u_proj, 2 * B * NP)
            sp.wait_ge(kv_done, B * NP)
            for b in range(B):
                sp.wait_ge(u_spilled[b], 16 * NP)

            def store(p, b, u):
                sp.wait_ge(y_ready, 2 * u + 2)
                sp.dma_start(out_v[b, bass.ds(p, 1)].rearrange("o i t c -> i (o t) c"), y[:, b]
                             ).then_inc(stored[b], 16)

            def phase2(p, last):
                for b in range(B):
                    u = unit(p, b)
                    load_x(p, b, u)
                    wait_for(sp, gated_ready, 2 * u)
                    sp.dma_start(u_in[:], u_dram[b, :, :, tokens(p)].rearrange("c p n -> p c n")
                                 ).then_inc(u_loaded, 16)
                    if not (last and b == 1):
                        load_q(*next_unit(p, b), u + 1)
                    if has_before(p, b):
                        store(*unit_before(p, b), u - 1)

            turns(sp, phase2)
            for j in range(2):
                sp.wait_ge(y_ready, 2 * (B * NP - 1) + j + 1)
                sp.dma_start(out_v[B - 1, NP - 1, :, 2 * j:2 * j + 2], y[:, B - 1, 2 * j:2 * j + 2]
                             ).then_inc(stored[B - 1], 16)
            sp.wait_ge(stored[0], 16 * NP)
            sp.wait_ge(stored[1], 16 * (NP + 1))

        @block.gpsimd
        def _(pool):
            nc.gpsimd.memset(neg_half[:], -0.5).then_inc(pool_step, 1)
            nc.gpsimd.memset(kv_acc[:], 0.0).then_inc(zeroed, 1)
            nc.gpsimd.memset(xn_t[:, :, :, 0:1], 0.0).then_inc(zeroed, 1)
            nc.gpsimd.memset(neg_one[:], -1.0).then_inc(pool_step, 1)
            nc.gpsimd.memset(eps[:], EPS).then_inc(pool_step, 1)
            pool.wait_ge(pool_step, 3)

            def rstd_of(b, ready, base):
                nc.gpsimd.tensor_tensor(rstd[:, b], mv[:, b, :, 1], eps[:], ALU.add).then_inc(pool_step, 1)
                nc.gpsimd.tensor_tensor(nmr[:, b], mv[:, b, :, 0], neg_one[:], ALU.mult).then_inc(pool_step, 1)
                pool.wait_ge(pool_step, base + 2)
                nc.gpsimd.tensor_tensor(rstd[:, b], rstd[:, b], neg_half[:], ALU.pow).then_inc(pool_step, 1)
                pool.wait_ge(pool_step, base + 3)
                nc.gpsimd.tensor_tensor(nmr[:, b], nmr[:, b], rstd[:, b], ALU.mult).then_inc(ready, 1)

            def rstd1(b, u):
                pool.wait_ge(mv_ready, u + 1)
                rstd_of(b, rstd_ready, 3 + 3 * u)

            for b in range(B):
                rstd1(b, b)
                pool.wait_ge(w_hi_ready, b + 1)
                for at, width in ((0, D), (D, D)) if b == 0 else ((0, 2 * D),):
                    cols_at = slice(2 * D * b + at, 2 * D * b + at + width)
                    nc.gpsimd.tensor_tensor(w_lo[:, :, cols_at], w_raw[:, b, :, at:at + width],
                                            w_hi[:, :, cols_at].bitcast(F32), ALU.subtract).then_inc(w_lo_ready, 1)
            pool.wait_ge(small_loaded, 16 * SMALL_LOADS)

            def phase1(p, last):
                for b in range(B):
                    u = unit(p, b)
                    for j in range(2):
                        pool.wait_ge(v_raw, 2 * u + j + 1)
                        nc.gpsimd.tensor_tensor(v_sb[:, 2 * j:2 * j + 2], v_sb[:, 2 * j:2 * j + 2],
                                                b_v_bc[:].unsqueeze(1).to_broadcast([P, 2, D]), ALU.add
                                                ).then_inc(v_ready, 1)
                    for c in range(C):
                        pool.wait_ge(q_ready, 2 * u + c + 1)
                        pool.wait_ge(rot_t_ready, 4 * p + 2 * c + 2)
                        cos_part, sin_part = (q_rot[:, 2 * c + s, b, tokens(p)] for s in range(2))
                        nc.gpsimd.tensor_tensor(cos_part, sin_part, rot_t[:, 2 * c], ALU.mult).then_inc(q_rot_ready, 1)
                        pool.wait_ge(q_rot_ready, 4 * u + 2 * c + 1)
                        nc.gpsimd.tensor_tensor(pool_tick[:], eps[:, 0:1], eps[:, 0:1], ALU.add)
                        nc.gpsimd.tensor_tensor(sin_part, sin_part, rot_t[:, 2 * c + 1], ALU.mult
                                                ).then_inc(q_rot_ready, 1)
                        if c == 0 and not last:
                            rstd1(b, u + 2)
                    if last and b == 0:
                        pool.wait_ge(rot_ready, 2 * NP)
                        nc.gpsimd.memset(kv_bd[:], 0.0).then_inc(kv_bd_zeroed, 1)
                        make_diff(0, 0, 0)
                if is_first(p):
                    pool.wait_ge(mix_hi_ready, 1)
                    nc.gpsimd.tensor_tensor(mix_lo[:], mix_raw, mix_hi[:].bitcast(F32), ALU.subtract
                                            ).then_inc(mix_lo_ready, 1)

            def make_diff(p, b, u):
                wait_for(pool, xr_raw_ready, u)
                nc.gpsimd.tensor_tensor(diff[:], xn_t[:, :, b, tokens(p, 1)], xn_t[:, :, b, tokens(p)],
                                        ALU.subtract).then_inc(diff_ready, 1)

            turns(pool, phase1)
            pool.wait_ge(xn_t_ready, B * NP)

            def xr_low(u):
                pool.wait_ge(xr_raw_ready, u + 1)
                pool.wait_ge(xr_split, 2 * u + 1)
                nc.gpsimd.tensor_tensor(xr_lo[:], x_mix[:], xr_hi[:].bitcast(F32), ALU.subtract).then_inc(xr_split, 1)

            xr_low(0)
            pool.wait_ge(bout_loaded, 16)

            def add_residual(b, u, j):
                pool.wait_ge(xb_ready, u + 1)
                pool.wait_ge(rv_ready, 2 * u + j + 1)
                nc.gpsimd.tensor_tensor(y[:, b, 2 * j:2 * j + 2], y[:, b, 2 * j:2 * j + 2],
                                        x_res[:, b, 2 * j:2 * j + 2], ALU.add).then_inc(y_part, 1)

            def phase2(p, last):
                for b in range(B):
                    u = unit(p, b)
                    end = last and b == 1
                    if not end and not attention_first(p, b):
                        make_diff(*next_unit(p, b), u + 1)
                    if has_before(p, b):
                        add_residual(1 - b, u - 1, 1)
                    pool.wait_ge(mv2_ready, u + 1)
                    rstd_of(b, rstd2_ready, 3 + 3 * B * NP + 3 * u)
                    if not end and attention_first(p, b):
                        make_diff(*next_unit(p, b), u + 1)
                    pool.wait_ge(res_loaded[b], 16 * (p + 1))
                    nc.gpsimd.tensor_tensor(x_res[:, b], x_res[:, b], b_out_bc[:].unsqueeze(1).to_broadcast([P, T, D]),
                                            ALU.add).then_inc(xb_ready, 1)
                    if not end:
                        xr_low(u + 1)
                    add_residual(b, u, 0)

            turns(pool, phase2)
            add_residual(B - 1, B * NP - 1, 1)

        @block.scalar
        def _(act):
            act.dma_start(const[:], consts).then_inc(consts_loaded, 16)
            act.dma_start(theta_bc[:], theta.to_broadcast([P, D])).then_inc(consts_loaded, 16)
            nc.scalar.preload_act_table_set("silu_and_others")
            act.dma_start(b_k_bc[:], b_qkvu[:, 0:D].to_broadcast([P, D])).then_inc(small_loaded, 16)
            act.dma_start(b_v_bc[:], b_qkvu[:, D:2 * D].to_broadcast([P, D])).then_inc(small_loaded, 16)
            col = lambda a: a.rearrange("o (c p) -> p (o c)", p=P)
            with nc.allow_non_contiguous_dma(reason="six columns of a few hundred bytes"):
                for dst, src in ((bq, col(b_qkvu[:, 2 * D:3 * D])), (bu, col(b_qkvu[:, 3 * D:4 * D])),
                                 (lnw, col(ln_w)), (lnb, col(ln_b)), (mur, col(mu_r)), (muk, col(mu_k))):
                    act.dma_start(dst, src).then_inc(small_loaded, 16)
            act.dma_start(b_out_bc[:], b_out.to_broadcast([P, D])).then_inc(bout_loaded, 16)

            def keep_xn_t(p, b, u):
                act.wait_ge(xn_transposed, u + 1)
                nc.scalar.activation(xn_t[:, :, b, tokens(p, 1)], xn_ps[:], ACT.Copy).then_inc(xn_t_ready, 1)

            def sin_cos(n):
                act.wait_ge(angle_step, ANGLE_STEPS * (n + 1))
                nc.scalar.activation(rot[:, 1], angle[:, 0], ACT.Sin).then_inc(rot_ready, 1)
                nc.scalar.activation(rot[:, 0], angle[:, 1], ACT.Sin, bias=half_pi[:], scale=-1.0).then_inc(rot_ready, 1)

            def keep_rot_t(p, g):
                act.wait_ge(rot_transposed, 4 * p + g + 1)
                wait_for(act, q_rot_ready, 8 * p)
                nc.scalar.activation(rot_t[:, g], rot_ps[:], ACT.Copy).then_inc(rot_t_ready, 1)

            def keep_q(p, b, u, c):
                act.wait_ge(q_proj, 2 * u + c + 1)
                nc.scalar.activation(q_rot[:, 2 * c + 1, b, tokens(p)], q_ps[:, c], ACT.Silu, bias=bq[:, c:c + 1]
                                     ).then_inc(q_ready, 1)

            def keep_u(p, b, u, c):
                act.wait_ge(u_proj, 2 * u + c + 1)
                wait_for(act, u_spilled[b], 16 * p)
                nc.scalar.activation(u_out[:, b, c], u_ps[:, c], ACT.Identity, bias=bu[:, c:c + 1]).then_inc(u_ready, 1)

            def split_xk(u):
                act.wait_ge(xk_raw_ready, u + 1)
                wait_for(act, kf_done, 2 * u)
                nc.scalar.activation(xk_hi[:], x_mix[:], ACT.Copy).then_inc(xk_split, 1)

            for i in range(2):
                act.wait_ge(w_loaded[i], 16)
                half = slice(i * 2 * D, (i + 1) * 2 * D)
                nc.scalar.activation(w_hi[:, :, half], w_raw[:, i], ACT.Copy).then_inc(w_hi_ready, 1)
                if i == 0:
                    act.wait_ge(zeroed, 3)
                    H = BLK // 2
                    act.wait_ge(half_turned, 1)
                    nc.scalar.activation(xn_t[:, :, 0, 1:1 + H], xn_ps[:, :, 0:H], ACT.Copy).then_inc(half_kept, 1)
                    act.wait_ge(xn_transposed, 1)
                    nc.scalar.activation(xn_t[:, :, 0, 1 + H:1 + BLK], q_ps[:, :, 0:H], ACT.Copy).then_inc(xn_t_ready, 1)
            act.wait_ge(small_loaded, 16 * SMALL_LOADS)

            def phase1(p, last):
                for b in range(B):
                    u = unit(p, b)
                    for j in range(2):
                        act.wait_ge(k_biased, 2 * u + j + 1)
                        nc.scalar.activation(k_sb[:, 2 * j:2 * j + 2], k_sb[:, 2 * j:2 * j + 2], ACT.Silu
                                             ).then_inc(k_silu_ready, 1)
                        act.wait_ge(v_proj, 2 * u + j + 1)
                        wait_for(act, kv_done, u)
                        nc.scalar.activation(v_sb[:, 2 * j:2 * j + 2], v_ps[:].rearrange("p (t n) -> p t n", t=2),
                                             ACT.Copy).then_inc(v_raw, 1)
                        if is_first(u) and j == 0:
                            sin_cos(0)
                    if not (last and b == 1):
                        keep_xn_t(*next_unit(p, b), u + 1)
                    if b == 0:
                        keep_rot_t(p, 0)
                    if last and b == 1:
                        act.wait_ge(mix_lo_ready, 1)
                    keep_q(p, b, u, 0)
                    if b == 0:
                        keep_rot_t(p, 1)
                    keep_q(p, b, u, 1)
                    if b == 0:
                        keep_rot_t(p, 2)
                    if last and b == 1:
                        split_xk(0)
                    keep_u(p, b, u, 0)
                    if b == 0:
                        keep_rot_t(p, 3)
                    keep_u(p, b, u, 1)
                    if is_first(u):
                        act.wait_ge(mix_loaded, 16 * 4)
                        nc.scalar.activation(mix_raw[:, 2], mix_raw[:, 2], ACT.Copy, scale=0.5).then_inc(mix_halved, 1)
                        act.wait_ge(mix_halved, 1)
                        nc.scalar.activation(mix_hi[:], mix_raw, ACT.Copy).then_inc(mix_hi_ready, 1)
                if not last:
                    act.wait_ge(k_rot_ready, 2 * unit(p, 1) + 2)
                    sin_cos(p + 1)

            turns(act, phase1)

            def split_xr(u):
                act.wait_ge(xr_raw_ready, u + 1)
                wait_for(act, r_done, 2 * u)
                nc.scalar.activation(xr_hi[:], x_mix[:], ACT.Copy).then_inc(xr_split, 1)

            def gate(p, b, u, j):
                act.wait_ge(r_done, 2 * u + j + 1)
                if is_first(p):
                    act.wait_ge(q_rot_ready, 4 * B * NP)
                wait_for(act, stored[b], 16 * p)
                nc.scalar.activation(y[:, b, 2 * j:2 * j + 2], r_ps[j][:].rearrange("p (t n) -> p t n", t=2),
                                     ACT.Tanh, scale=0.5).then_inc(tanh_ready, 1)

            def split_gated(u):
                for c in range(C):
                    act.wait_ge(gated_ready, 2 * u + c + 1)
                    wait_for(act, w_done, 2 * u)
                    nc.scalar.activation(g_hi[:, c], gated[:, c], ACT.Copy).then_inc(g_hi_ready, 1)

            def phase2(p, last):
                for b in range(B):
                    u = unit(p, b)
                    end = last and b == 1

                    def normalise():
                        act.wait_ge(rstd2_ready, u + 1)
                        wait_for(act, z_transposed, 2 * u)
                        for t in range(T):
                            ins = nc.scalar.activation(z[:, t], o_ps[:, t // 2, (t % 2) * D:(t % 2 + 1) * D],
                                                       ACT.Identity, bias=nmr[:, b, t:t + 1], scale=rstd[:, b, t:t + 1])
                        ins.then_inc(z_ready, 1)

                    if has_before(p, b) and attention_first(p, b):
                        split_gated(u - 1)
                    for c in range(C):
                        act.wait_ge(kf_done, 2 * u + c + 1)
                        wait_for(act, ka_lo_ready, 2 * u + c)
                        nc.scalar.activation(k_act[:], kf_ps[:], ACT.Relu).then_inc(relu_done, 1)
                        act.wait_ge(relu_done, 2 * u + c + 1)
                        wait_for(act, vf_done, 2 * u)
                        nc.scalar.activation(ka_hi[:, c], k_act[:], ACT.Square).then_inc(ka_hi_ready, 1)
                        act.wait_ge(ka_hi_ready, 2 * u + c + 1)
                        nc.scalar.activation(k_act[:], k_act[:], ACT.Square).then_inc(k_sq_ready, 1)
                        if c == 0 and has_before(p, b) and not attention_first(p, b):
                            split_gated(u - 1)
                        if c == 0 and attention_first(p, b):
                            normalise()
                    gate(p, b, u, 0)
                    if not end and not attention_first(p, b):
                        split_xk(u + 1)
                    if not attention_first(p, b):
                        normalise()
                    gate(p, b, u, 1)
                    if not end and attention_first(p, b):
                        split_xk(u + 1)
                    if not end:
                        split_xr(u + 1)
                    for c in range(C):
                        act.wait_ge(z_transposed, 2 * u + c + 1)
                        wait_for(act, g_lo_ready, 2 * u)
                        nc.scalar.activation(gated[:, c], z_ps[:, c], ACT.Identity, bias=lnb[:, c:c + 1],
                                             scale=lnw[:, c:c + 1]).then_inc(aff_ready, 1)

            split_xr(0)
            turns(act, phase2)
            split_gated(B * NP - 1)

        @block.vector
        def _(dve):
            nc.vector.memset(half_pi[:], float(np.float32(np.pi / 2))).then_inc(zeroed, 1)

            def stats1(p, b, u):
                dve.wait_ge(x_loaded[b], 16 * (p + 1))
                for t in range(T):
                    nc.vector.bn_stats(stats[:, t], x_in[:, b, t]).then_inc(stats_ready, 1)
                dve.wait_ge(stats_ready, T * (u + 1))
                nc.vector.memset(tick[:], 0.0)
                for t in range(T):
                    ins = nc.vector.bn_aggr(mv[:, b, t], stats[:, t])
                ins.then_inc(mv_ready, 1)

            def norm1(b, u):
                dve.wait_ge(rstd_ready, u + 1)
                for t in range(T):
                    nc.vector.tensor_scalar(x_in[:, b, t], x_in[:, b, t], mv[:, b, t, 0:1], rstd[:, b, t:t + 1],
                                            ALU.subtract, ALU.mult).then_inc(xn_ready, 1)

            def split(p, b, u):
                dve.wait_ge(xn_t_ready, u + 1)
                wait_for(dve, u_proj, 2 * (u - 1))
                nc.vector.tensor_copy(xn_hi[:, b], xn_t[:, :, b, tokens(p, 1)]).then_inc(split_ready, 1)
                dve.wait_ge(split_ready, 2 * u + 1)
                nc.vector.tensor_tensor(xn_lo[:, b], xn_t[:, :, b, tokens(p, 1)], xn_hi[:, b].bitcast(F32),
                                        ALU.subtract).then_inc(split_ready, 1)

            def angles(n, first, end):
                a, k = angle[:, 0], angle[:, 1]
                for i in range(first, end):
                    if i == 0:
                        wait_for(dve, rot_ready, 2 * n)
                        ins = nc.vector.tensor_tensor(a, theta_bc[:].unsqueeze(1).to_broadcast([P, T, D]),
                                                      pos[:, bass.ds(n * T, T)].unsqueeze(2).to_broadcast([P, T, D]),
                                                      ALU.mult)
                    else:
                        dve.wait_ge(angle_step, ANGLE_STEPS * n + i)
                    if i == 1:
                        ins = nc.vector.tensor_scalar(k, a, INV_TWO_PI, ROUND, ALU.mult, ALU.add)
                    if i == 2:
                        ins = nc.vector.tensor_scalar(k, k, -ROUND, None, ALU.add)
                    if i == 3:
                        ins = nc.vector.scalar_tensor_tensor(a, k, -TWO_PI_HI, a, ALU.mult, ALU.add)
                    if i == 4:
                        ins = nc.vector.scalar_tensor_tensor(a, k, -TWO_PI_LO, a, ALU.mult, ALU.add)
                    if i == 5:
                        ins = nc.vector.tensor_scalar(a, a, PI_BELOW, -PI_BELOW, ALU.min, ALU.max)
                    if i == 6:
                        ins = nc.vector.tensor_scalar(k.bitcast(U32), a.bitcast(U32), 0x7FFFFFFF, None, ALU.bitwise_and)
                    ins.then_inc(angle_step, 1)

            def add_bias_k(u, j):
                dve.wait_ge(k_proj, 2 * u + j + 1)
                wait_for(dve, k_rot_ready, 2 * u)
                nc.vector.tensor_tensor(k_sb[:, 2 * j:2 * j + 2], k_ps[:].rearrange("p (t n) -> p t n", t=2),
                                        b_k_bc[:].unsqueeze(1).to_broadcast([P, 2, D]), ALU.add).then_inc(k_biased, 1)

            def rotate_k(u, j, b):
                dve.wait_ge(k_silu_ready, 2 * u + j + 1)
                if j == 0:
                    wait_for(dve, kv_done, u)
                for cs in range(2):
                    ins = nc.vector.tensor_tensor(k_rot[:, 2 * j:2 * j + 2, cs], k_sb[:, 2 * j:2 * j + 2],
                                                  rot[:, cs, 2 * j:2 * j + 2], ALU.mult)
                ins.then_inc(k_rot_ready, 1)

            def add_kv(b, u):
                dve.wait_ge(kv_done, u + 1)
                nc.vector.tensor_tensor(kv_acc[:, b], kv_acc[:, b],
                                        kv_ps[:, 0:C * 2 * G].rearrange("p (c s g) -> p c s g", c=C, s=2),
                                        ALU.add).then_inc(kv_added, 1)

            stats1(0, 0, 0)
            dve.wait_ge(consts_loaded, 32)
            angles(0, 0, 1)
            norm1(0, 0)
            angles(0, 1, 2)
            H = BLK // 2
            for at, kept, ready in ((0, half_kept, half_split), (H, xn_t_ready, split_ready)):
                dve.wait_ge(kept, 1)
                xn, hi, lo = xn_t[:, :, 0, 1 + at:1 + at + H], xn_hi[:, 0, :, at:at + H], xn_lo[:, 0, :, at:at + H]
                nc.vector.tensor_copy(hi, xn).then_inc(ready, 1)
                dve.wait_ge(ready, 1)
                nc.vector.tensor_tensor(lo, xn, hi.bitcast(F32), ALU.subtract).then_inc(ready, 1)
            angles(0, 2, 3)
            stats1(0, 1, 1)
            angles(0, 3, 4)
            dve.wait_ge(small_loaded, 16 * SMALL_LOADS)
            add_bias_k(0, 0)
            angles(0, 4, ANGLE_STEPS)
            add_bias_k(0, 1)

            def phase1(p, last):
                for b in range(B):
                    u = unit(p, b)
                    end = last and b == 1
                    if not end:
                        norm1(next_unit(p, b)[1], u + 1)
                    for j in range(2):
                        if not is_first(u):
                            add_bias_k(u, j)
                        if b == 0 and j == 0:
                            dve.wait_ge(rot_ready, 2 * p + 2)
                        rotate_k(u, j, b)
                    if not end:
                        split(*next_unit(p, b), u + 1)
                    if not last:
                        stats1(p + 1, b, u + 2)
                        angles(p + 1, *((0, 4) if b == 0 else (4, ANGLE_STEPS)))
                    if end:
                        dve.wait_ge(kv_bd_zeroed, 1)
                        block_diagonal(0, rot_ps)
                        xk_raw(0, 0, 0)
                        dve.wait_ge(u_proj, 2 * B * NP)
                        xk_low(0)
                        xr_raw(0, 0, 0)
                    add_kv(b, u)

            def block_diagonal(b, turned):
                dve.wait_ge(kv_turned, b + 1)
                turned = turned[:, 0:C * P].rearrange("p (c e) -> p c e", c=C)
                for cs in range(2):
                    for h in range(2):
                        rows, src, e = slice(G * h, G * h + G), slice(G * cs, G * cs + G), slice(G * h, G * h + G)
                        ins = nc.vector.tensor_tensor(kv_bd[rows, b, cs, :, e], turned[src, :, e],
                                                      mask[src].unsqueeze(1).to_broadcast([G, C, G]), ALU.mult)
                ins.then_inc(kv_bd_ready, 1)

            def mixed(mu, p, b, u, ready):
                dve.wait_ge(diff_ready, u + 1)
                for c in range(C):
                    ins = nc.vector.scalar_tensor_tensor(x_mix[:, c], diff[:, c], mu[:, c:c + 1],
                                                         xn_t[:, c, b, tokens(p)], ALU.mult, ALU.add)
                ins.then_inc(ready, 1)

            def xk_raw(p, b, u):
                wait_for(dve, xr_split, 2 * u)
                mixed(muk, p, b, u, xk_raw_ready)

            def xk_low(u):
                dve.wait_ge(xk_split, 2 * u + 1)
                nc.vector.tensor_tensor(xk_lo[:], x_mix[:], xk_hi[:].bitcast(F32), ALU.subtract).then_inc(xk_split, 1)

            def xr_raw(p, b, u):
                dve.wait_ge(xk_split, 2 * u + 2)
                mixed(mur, p, b, u, xr_raw_ready)

            def ka_low(u, c):
                dve.wait_ge(k_sq_ready, 2 * u + c + 1)
                nc.vector.tensor_tensor(ka_lo[:, c], k_act[:], ka_hi[:, c].bitcast(F32), ALU.subtract
                                        ).then_inc(ka_lo_ready, 1)

            def gated_low(u):
                for c in range(C):
                    dve.wait_ge(g_hi_ready, 2 * u + c + 1)
                    nc.vector.tensor_tensor(g_lo[:, c], gated[:, c], g_hi[:, c].bitcast(F32), ALU.subtract
                                            ).then_inc(g_lo_ready, 1)

            def finish(p, b, u, j):
                dve.wait_ge(w_done, 2 * u + j + 1)
                dve.wait_ge(y_part, 2 * u + j + 1)
                nc.vector.tensor_tensor(y[:, b, 2 * j:2 * j + 2], w_ps[j][:].rearrange("p (t n) -> p t n", t=2),
                                        y[:, b, 2 * j:2 * j + 2], ALU.add).then_inc(y_ready, 1)

            turns(dve, phase1)

            def phase2(p, last):
                for b in range(B):
                    u = unit(p, b)
                    end = last and b == 1

                    def gate_v(j):
                        dve.wait_ge(vf_done, 2 * u + j + 1)
                        dve.wait_ge(tanh_ready, 2 * u + j + 1)
                        nc.vector.scalar_tensor_tensor(y[:, b, 2 * j:2 * j + 2], y[:, b, 2 * j:2 * j + 2], 1.0,
                                                       vf_ps[j][:].rearrange("p (t n) -> p t n", t=2),
                                                       ALU.add, ALU.mult).then_inc(rv_ready, 1)

                    for j in range(2):
                        if j == 0 and not attention_first(p, b):
                            ka_low(u, 0)
                        dve.wait_ge(o_done, 2 * u + j + 1)
                        for i in range(2):
                            nc.vector.bn_stats(stats[:, 2 * j + i], o_ps[:, j, i * D:(i + 1) * D]).then_inc(stats_ready, 1)
                        if j == 0 and has_before(p, b) and not attention_first(p, b):
                            gated_low(u - 1)
                    dve.wait_ge(stats_ready, T * (B * NP + u + 1))
                    nc.vector.memset(tick[:], 0.0)
                    for t in range(T):
                        ins = nc.vector.bn_aggr(mv[:, b, t], stats[:, t])
                    ins.then_inc(mv2_ready, 1)
                    if attention_first(p, b):
                        if has_before(p, b):
                            gated_low(u - 1)
                        ka_low(u, 0)
                        if not end:
                            xk_raw(*next_unit(p, b), u + 1)
                        ka_low(u, 1)
                    else:
                        ka_low(u, 1)
                        xk_raw(*next_unit(p, b), u + 1)
                    if is_first(u):
                        block_diagonal(1, w_ps[0])
                    if has_before(p, b):
                        finish(*unit_before(p, b), u - 1, 0)
                    if not end:
                        xk_low(u + 1)
                    if has_before(p, b):
                        finish(*unit_before(p, b), u - 1, 1)
                    if not end:
                        xr_raw(*next_unit(p, b), u + 1)
                    def gate_u():
                        for c in range(C):
                            dve.wait_ge(aff_ready, 2 * u + c + 1)
                            if c == 0:
                                dve.wait_ge(u_loaded, 16 * (u + 1))
                            nc.vector.tensor_tensor(gated[:, c], gated[:, c], u_in[:, c], ALU.mult).then_inc(gated_ready, 1)

                    if end:
                        gate_u()
                        gated_low(u)
                    gate_v(0)
                    gate_v(1)
                    if not end:
                        gate_u()

            turns(dve, phase2)
            for j in range(2):
                finish(NP - 1, B - 1, B * NP - 1, j)

        @block.tensor
        def _(pe):
            K0, V0, Q0, U0 = 0, D, 2 * D, 3 * D

            def turn_xn(b, u):
                wait_for(pe, xn_t_ready, u)
                wait_for(pe, u_ready, 2 * (u - 1))
                for t in range(T):
                    pe.wait_ge(xn_ready, T * u + t + 1)
                    for c in range(C):
                        ins = nc.tensor.transpose(xn_ps[:, c, t * P:(t + 1) * P], x_in[:, b, t, c * P:(c + 1) * P], ident)
                ins.then_inc(xn_transposed, 1)

            def tile_pair(ps, b, j, w0):
                for i in range(2):
                    t = 2 * j + i
                    for c in range(C):
                        for x_part, w_part in ((xn_hi, w_hi), (xn_hi, w_lo), (xn_lo, w_hi)):
                            ins = nc.tensor.matmul(ps[:, i * D:(i + 1) * D], x_part[:, b, c, t * P:(t + 1) * P],
                                                   w_part[:, c, w0:w0 + D],
                                                   start=c == 0 and x_part is xn_hi and w_part is w_hi,
                                                   stop=c == C - 1 and x_part is xn_lo)
                return ins

            def channels(ps, b, w0):
                for c in range(C):
                    for w_part, x_part in ((w_hi, xn_hi), (w_lo, xn_hi), (w_hi, xn_lo)):
                        ins = nc.tensor.matmul(ps, w_part[:, c, w0:w0 + P], x_part[:, b, c],
                                               start=c == 0 and w_part is w_hi and x_part is xn_hi,
                                               stop=c == C - 1 and x_part is xn_lo)
                return ins

            def turn_kv(b, ps):
                pe.wait_ge(kv_added, 2 * NP - 1 + b)
                for c in range(C):
                    ins = nc.tensor.transpose(ps[:, c * P:(c + 1) * P],
                                              kv_acc[:, b, c].rearrange("p s g -> p (s g)"), ident)
                ins.then_inc(kv_turned, 1)

            def turn_rot(p, g):
                wait_for(pe, rot_t_ready, 4 * p + g)
                for t in range(T):
                    ins = nc.tensor.transpose(rot_ps[:, t * P:(t + 1) * P], rot[:, g % 2, t, g // 2 * P:(g // 2 + 1) * P], ident)
                ins.then_inc(rot_transposed, 1)

            pe.wait_ge(consts_loaded, 32)
            for t in range(T):
                pe.wait_ge(xn_ready, t + 1)
                for c in range(C):
                    ps = (xn_ps, q_ps)[t // 2]
                    ins = nc.tensor.transpose(ps[:, c, t % 2 * P:(t % 2 + 1) * P], x_in[:, 0, t, c * P:(c + 1) * P], ident)
                if t % 2:
                    ins.then_inc((half_turned, xn_transposed)[t // 2], 1)
            pe.wait_ge(w_hi_ready, 1)
            pe.wait_ge(w_lo_ready, 1)

            def phase1(p, last):
                for b in range(B):
                    u = unit(p, b)
                    for j in range(2):
                        if is_first(u) and j == 0:
                            pe.wait_ge(half_split, 2)
                        else:
                            pe.wait_ge(split_ready, 2 * u + 2)
                        wait_for(pe, k_biased, 2 * u + j)
                        tile_pair(k_ps, b, j, K0).then_inc(k_proj, 1)
                        if is_first(u):
                            pe.wait_ge(w_lo_ready, 2)
                        wait_for(pe, v_raw, 2 * u + j)
                        tile_pair(v_ps, b, j, V0).then_inc(v_proj, 1)
                    if not (last and b == 1):
                        turn_xn(next_unit(p, b)[1], u + 1)
                    else:
                        pe.wait_ge(rot_t_ready, 4 * NP)
                        turn_kv(0, rot_ps)
                    if b == 0:
                        pe.wait_ge(rot_ready, 2 * p + 2)
                        turn_rot(p, 0)
                    pe.wait_ge(w_hi_ready, 2)
                    pe.wait_ge(w_lo_ready, 3)
                    for c in range(C):
                        wait_for(pe, q_ready, 2 * u)
                        channels(q_ps[:, c], b, Q0 + c * P).then_inc(q_proj, 1)
                        if b == 0:
                            turn_rot(p, 1 + c)
                    for c in range(C):
                        if last and b == 1:
                            pe.wait_ge(u_ready, 2 * u)
                        else:
                            pe.wait_ge(xn_t_ready, u + 2)
                        channels(u_ps[:, c], b, U0 + c * P).then_inc(u_proj, 1)
                        if b == 0 and c == 0:
                            turn_rot(p, 3)
                    pe.wait_ge(v_ready, 2 * u + 2)
                    pe.wait_ge(k_rot_ready, 2 * u + 2)
                    wait_for(pe, kv_added, u)
                    for t in range(T):
                        for c in range(C):
                            for h in range(2):
                                d0 = c * P + h * G
                                ins = nc.tensor.matmul(
                                    kv_ps[h * G:(h + 1) * G, c * 2 * G:(c + 1) * 2 * G],
                                    v_sb[:, t, d0:d0 + G], k_rot[:, t, :, d0:d0 + G],
                                    start=t == 0 and c == 0, stop=t == T - 1, skip_group_check=True)
                    ins.then_inc(kv_done, 1)

            turns(pe, phase1)
            pe.wait_ge(u_ready, 2 * B * NP)

            W_R, W_K, W_V, W_O = range(4)

            def rows(ps, x_hi, x_lo, w, j):
                for i in range(2):
                    t = 2 * j + i
                    for c in range(C):
                        for x_part, w_part in ((x_hi, mix_hi), (x_hi, mix_lo), (x_lo, mix_hi)):
                            ins = nc.tensor.matmul(ps[:, i * D:(i + 1) * D], x_part[:, c, t * P:(t + 1) * P],
                                                   w_part[:, w, c],
                                                   start=c == 0 and x_part is x_hi and w_part is mix_hi,
                                                   stop=c == C - 1 and x_part is x_lo)
                return ins

            pe.wait_ge(mix_hi_ready, 1)
            pe.wait_ge(mix_lo_ready, 1)

            def project(u, j):
                pe.wait_ge(g_hi_ready, 2 * u + 2)
                pe.wait_ge(g_lo_ready, 2 * u + 2)
                wait_for(pe, y_ready, 2 * u)
                rows(w_ps[j], g_hi, g_lo, W_O, j).then_inc(w_done, 1)

            def phase2(p, last):
                for b in range(B):
                    u = unit(p, b)

                    def attend(j):
                        if j == 0:
                            pe.wait_ge(q_loaded[b], 16 * (p + 1))
                            wait_for(pe, z_ready, u)
                        for i in range(2):
                            t = 2 * j + i
                            for c in range(C):
                                for cs in range(2):
                                    ins = nc.tensor.matmul(o_ps[:, j, i * D + c * P:i * D + (c + 1) * P],
                                                           q_in[:, b, 2 * c + cs, t * P:(t + 1) * P],
                                                           kv_bd[:, b, cs, c], start=cs == 0, stop=cs == 1)
                        ins.then_inc(o_done, 1)

                    def mix_k(o):
                        pe.wait_ge(xk_split, 2 * u + 2)
                        wait_for(pe, relu_done, 2 * u + o)
                        for c in range(C):
                            for w_part, x_part in ((mix_hi, xk_hi), (mix_lo, xk_hi), (mix_hi, xk_lo)):
                                ins = nc.tensor.matmul(kf_ps[:], w_part[:, W_K, c, o * P:(o + 1) * P], x_part[:, c],
                                                       start=c == 0 and w_part is mix_hi and x_part is xk_hi,
                                                       stop=c == C - 1 and x_part is xk_lo)
                        ins.then_inc(kf_done, 1)

                    def mix_r(j):
                        pe.wait_ge(xr_split, 2 * u + 2)
                        wait_for(pe, rv_ready, 2 * u)
                        if j == 1:
                            wait_for(pe, aff_ready, 2 * u)
                        rows(r_ps[j], xr_hi, xr_lo, W_R, j).then_inc(r_done, 1)

                    def mix_v(j):
                        if j == 0:
                            wait_for(pe, rv_ready, 2 * u)
                        else:
                            pe.wait_ge(tanh_ready, 2 * u + 1)
                        rows(vf_ps[j], ka_hi, ka_lo, W_V, j).then_inc(vf_done, 1)

                    def turn_z():
                        pe.wait_ge(z_ready, u + 1)
                        for c in range(C):
                            if c == 0:
                                pe.wait_ge(tanh_ready, 2 * u + 2)
                            else:
                                wait_for(pe, y_ready, 2 * u)
                            for t in range(T):
                                ins = nc.tensor.transpose(z_ps[:, c, t * P:(t + 1) * P], z[:, t, c * P:(c + 1) * P],
                                                          ident)
                            ins.then_inc(z_transposed, 1)

                    def project_before(j):
                        if has_before(p, b):
                            project(u - 1, j)

                    if is_first(p):
                        pe.wait_ge(kv_bd_ready, b + 1)
                    if attention_first(p, b):
                        attend(0)
                        attend(1)
                        mix_k(0)
                        mix_r(0)
                        mix_k(1)
                        project_before(0)
                    else:
                        for j in range(2):
                            mix_k(j)
                            attend(j)
                        mix_r(0)
                        project_before(0)
                    if is_first(u):
                        turn_kv(1, w_ps[0])
                    mix_r(1)
                    project_before(1)
                    if attention_first(p, b):
                        turn_z()
                    pe.wait_ge(ka_hi_ready, 2 * u + 2)
                    pe.wait_ge(ka_lo_ready, 2 * u + 2)
                    mix_v(0)
                    mix_v(1)
                    if not attention_first(p, b):
                        turn_z()

            turns(pe, phase2)
            for j in range(2):
                project(B * NP - 1, j)


def kernel(L0_attn_x, L0_attn_context, L0_attn_Wqkvu, L0_attn_bqkvu, L0_attn_Wout, L0_attn_bout, L0_attn_theta,
           L0_attn_ln_w, L0_attn_ln_b, L0_ffn_W_r, L0_ffn_W_k, L0_ffn_W_v, L0_ffn_mu_r, L0_ffn_mu_k):
    import concourse.bacc as bacc
    from concourse.bass_utils import run_bass_kernel_spmd

    x = np.ascontiguousarray(L0_attn_x)
    d = x.shape[2]
    order = [1, 2, 0, 3]
    w = np.asarray(L0_attn_Wqkvu).reshape(4, d, d)
    bias = np.asarray(L0_attn_bqkvu).reshape(4, d)
    n_tiles = x.shape[1] // P
    p_i = np.arange(P)[:, None]
    identity = (p_i == np.arange(P)[None, :]).astype(np.float32)
    mask = (p_i % 64 // 16 == np.arange(64)[None, :] // 16).astype(np.float32)
    positions = (p_i + P * np.arange(n_tiles)[None, :]).astype(np.float32)
    row = lambda a: np.ascontiguousarray(np.asarray(a).reshape(1, -1))
    arrays = {
        "x": x,
        "w_qkvu_t": np.ascontiguousarray(np.stack([w[i] for i in order]).reshape(4 * d, d).T),
        "b_qkvu": row(np.stack([bias[i] for i in order])),
        "w_out_t": np.ascontiguousarray(np.asarray(L0_attn_Wout).T),
        "b_out": row(L0_attn_bout),
        "theta": row(L0_attn_theta),
        "ln_w": row(L0_attn_ln_w),
        "ln_b": row(L0_attn_ln_b),
        "w_r_t": np.ascontiguousarray(np.asarray(L0_ffn_W_r).T),
        "w_k_t": np.ascontiguousarray(np.asarray(L0_ffn_W_k).T),
        "w_v_t": np.ascontiguousarray(np.asarray(L0_ffn_W_v).T),
        "mu_r": row(L0_ffn_mu_r),
        "mu_k": row(L0_ffn_mu_k),
        "consts": np.concatenate([identity, mask, positions], axis=1),
    }
    nc = bacc.Bacc("TRN2", target_bir_lowering=False, num_devices=1)
    args = [nc.dram_tensor(n, a.shape, mybir.dt.from_np(a.dtype), kind="ExternalInput").ap() for n, a in arrays.items()]
    out = nc.dram_tensor("out", x.shape, mybir.dt.from_np(x.dtype), kind="ExternalOutput").ap()
    lrpe_block_kernel(nc, *args, out)
    result = run_bass_kernel_spmd(nc, [arrays], core_ids=[0])
    return result.results[0]["out"]
```
